# Optimizing a Trainium2 kernel written in Bass

```python
import numpy as np
import jax
import jax.numpy as jnp

def _softmax(x, axis=-1):
    return jax.nn.softmax(x, axis=axis)

def _gelu(x):
    return jax.nn.gelu(x, approximate=True)

def _silu(x):
    return jax.nn.silu(x)

def _sigmoid(x):
    return jax.nn.sigmoid(x)

def _layernorm(x, axis=-1, eps=1e-05):
    m = jnp.mean(x, axis=axis, keepdims=True)
    v = jnp.var(x, axis=axis, keepdims=True)
    return (x - m) / jnp.sqrt(v + eps)

def _scatter_add(tgt, idx, src, axis=0):
    return tgt.at[idx].add(src)

def _segment_sum(src, seg, n):
    return jax.ops.segment_sum(src, seg, n)
kernel_name = 'mk_seq_postln_d1_jaxref_r2_eba977'

def setup_inputs(seed: int=0):
    np.random.seed(seed)
    _w = jnp.asarray

    def _L0_attn_setup():
        import jax, jax.numpy as jnp
        import numpy as np
        D_MODEL = 512
        N_HEADS = 16
        NUM_PATTERN = 32
        HEAD_DIM = D_MODEL // N_HEADS

        def sparsemax(z):
            S = z.shape[-1]
            z_sorted = -jnp.sort(-z, axis=-1)
            cum = jnp.cumsum(z_sorted, axis=-1)
            k = jnp.arange(1, S + 1, dtype=z.dtype)
            support = 1.0 + k * z_sorted > cum
            k_sup = jnp.sum(support, axis=-1, keepdims=True)
            cum_sel = jnp.take_along_axis(cum, k_sup - 1, axis=-1)
            tau = (cum_sel - 1.0) / k_sup.astype(z.dtype)
            return jnp.maximum(z - tau, 0.0)
        key = jax.random.key(seed)
        ks = jax.random.split(key, 10)
        s = 1.0 / np.sqrt(D_MODEL)
        inp = {'query': jax.random.normal(ks[0], (8, 2048, D_MODEL), dtype=jnp.float32), 'key_param': jax.random.normal(ks[1], (1, NUM_PATTERN, D_MODEL), dtype=jnp.float32), 'Wq': jax.random.normal(ks[2], (D_MODEL, N_HEADS * HEAD_DIM), dtype=jnp.float32) * s, 'bq': jnp.zeros((N_HEADS * HEAD_DIM,), dtype=jnp.float32), 'Wk': jax.random.normal(ks[3], (D_MODEL, N_HEADS * HEAD_DIM), dtype=jnp.float32) * s, 'bk': jnp.zeros((N_HEADS * HEAD_DIM,), dtype=jnp.float32), 'Wv': jax.random.normal(ks[4], (N_HEADS * HEAD_DIM, N_HEADS * HEAD_DIM), dtype=jnp.float32) * s, 'bv': jnp.zeros((N_HEADS * HEAD_DIM,), dtype=jnp.float32), 'Wo': jax.random.normal(ks[5], (N_HEADS * HEAD_DIM, D_MODEL), dtype=jnp.float32) * s, 'bo': jnp.zeros((D_MODEL,), dtype=jnp.float32)}
        return inp
    _L0_attn_in = _L0_attn_setup()

    def _L0_ffn_setup():
        import jax, jax.numpy as jnp
        import numpy as np
        D_MODEL = 512
        M = 64
        INNER = 16
        key = jax.random.key(seed)
        ks = jax.random.split(key, 9)

        def init(k, shape, fan_in):
            bound = 1.0 / np.sqrt(fan_in)
            return jax.random.uniform(k, shape, jnp.float32, -bound, bound)
        x = jax.random.normal(ks[0], (16, 2048, D_MODEL), dtype=jnp.float32)
        Win = init(ks[1], (D_MODEL, M), D_MODEL)
        bin_ = init(ks[2], (M,), D_MODEL)
        W1 = init(ks[3], (M, INNER), 1)
        b1 = init(ks[4], (M, INNER), 1)
        W2 = init(ks[5], (M, INNER), INNER)
        b2 = init(ks[6], (M,), INNER)
        Wout = init(ks[7], (M, D_MODEL), M)
        bout = init(ks[8], (D_MODEL,), M)
        return {'x': x, 'Win': Win, 'bin_': bin_, 'W1': W1, 'b1': b1, 'W2': W2, 'b2': b2, 'Wout': Wout, 'bout': bout}
    _L0_ffn_in = _L0_ffn_setup()
    _d = {'L0_attn_query': _L0_attn_in['query'], 'L0_attn_key_param': _L0_attn_in['key_param'], 'L0_attn_Wq': _L0_attn_in['Wq'], 'L0_attn_bq': _L0_attn_in['bq'], 'L0_attn_Wk': _L0_attn_in['Wk'], 'L0_attn_bk': _L0_attn_in['bk'], 'L0_attn_Wv': _L0_attn_in['Wv'], 'L0_attn_bv': _L0_attn_in['bv'], 'L0_attn_Wo': _L0_attn_in['Wo'], 'L0_attn_bo': _L0_attn_in['bo'], 'L0_ffn_Win': _L0_ffn_in['Win'], 'L0_ffn_bin_': _L0_ffn_in['bin_'], 'L0_ffn_W1': _L0_ffn_in['W1'], 'L0_ffn_b1': _L0_ffn_in['b1'], 'L0_ffn_W2': _L0_ffn_in['W2'], 'L0_ffn_b2': _L0_ffn_in['b2'], 'L0_ffn_Wout': _L0_ffn_in['Wout'], 'L0_ffn_bout': _L0_ffn_in['bout']}
    _x0 = _d['L0_attn_query']
    _d['L0_attn_query'] = jax.random.normal(jax.random.fold_in(jax.random.key(seed), 1), (16, 1024, 512), dtype=_x0.dtype)
    del _x0
    return _d

def reference(L0_attn_query, L0_attn_key_param, L0_attn_Wq, L0_attn_bq, L0_attn_Wk, L0_attn_bk, L0_attn_Wv, L0_attn_bv, L0_attn_Wo, L0_attn_bo, L0_ffn_Win, L0_ffn_bin_, L0_ffn_W1, L0_ffn_b1, L0_ffn_W2, L0_ffn_b2, L0_ffn_Wout, L0_ffn_bout):

    def _L0_attn_ref(query, key_param, Wq, bq, Wk, bk, Wv, bv, Wo, bo):
        import jax, jax.numpy as jnp
        import numpy as np
        D_MODEL = 512
        N_HEADS = 16
        NUM_PATTERN = 32
        HEAD_DIM = D_MODEL // N_HEADS

        def sparsemax(z):
            S = z.shape[-1]
            z_sorted = -jnp.sort(-z, axis=-1)
            cum = jnp.cumsum(z_sorted, axis=-1)
            k = jnp.arange(1, S + 1, dtype=z.dtype)
            support = 1.0 + k * z_sorted > cum
            k_sup = jnp.sum(support, axis=-1, keepdims=True)
            cum_sel = jnp.take_along_axis(cum, k_sup - 1, axis=-1)
            tau = (cum_sel - 1.0) / k_sup.astype(z.dtype)
            return jnp.maximum(z - tau, 0.0)
        B, L, _ = query.shape
        S = key_param.shape[1]
        H, E = (N_HEADS, HEAD_DIM)
        D = HEAD_DIM
        k = jnp.broadcast_to(key_param, (B, S, D_MODEL))
        queries = (query @ Wq + bq).reshape(B, L, H, E)
        keys_flat = k @ Wk + bk
        values = (keys_flat @ Wv + bv).reshape(B, S, H, D)
        keys = keys_flat.reshape(B, S, H, E)
        scale = 1.0 / np.sqrt(E)
        scores = jnp.einsum('blhe,bshe->bhls', queries, keys)
        A = sparsemax(scale * scores)
        out = jnp.einsum('bhls,bshd->blhd', A, values)
        out = jnp.transpose(out, (0, 2, 1, 3)).reshape(B, L, H * D)
        return out @ Wo + bo

    def _L0_ffn_ref(x, Win, bin_, W1, b1, W2, b2, Wout, bout):
        import jax, jax.numpy as jnp
        import numpy as np
        D_MODEL = 512
        M = 64
        INNER = 16
        s = jnp.einsum('btd,dm->btm', x, Win) + bin_
        h = jax.nn.relu(s[..., None] * W1 + b1)
        g = jnp.einsum('btmh,mh->btm', h, W2) + b2
        out = jnp.einsum('btm,md->btd', g, Wout) + bout
        return out
    x = L0_attn_query
    x = _layernorm(x + _L0_attn_ref(x, L0_attn_key_param, L0_attn_Wq, L0_attn_bq, L0_attn_Wk, L0_attn_bk, L0_attn_Wv, L0_attn_bv, L0_attn_Wo, L0_attn_bo), axis=-1)
    x = _layernorm(x + _L0_ffn_ref(x, L0_ffn_Win, L0_ffn_bin_, L0_ffn_W1, L0_ffn_b1, L0_ffn_W2, L0_ffn_b2, L0_ffn_Wout, L0_ffn_bout), axis=-1)
    return x

_drawn_inputs = setup_inputs


def setup_inputs(seed=0):
    import zlib

    import numpy as np

    out = dict(_drawn_inputs(seed))
    spreads = {'L0_attn_bq': (0.0, 0.1),
     'L0_attn_bk': (0.0, 0.1),
     'L0_attn_bv': (0.0, 0.1),
     'L0_attn_bo': (0.0, 0.1)}
    factors = {'L0_ffn_bin_': 8.0}
    for name, (base, spread) in spreads.items():
        noise = np.random.default_rng([zlib.crc32(name.encode()), seed]).standard_normal(out[name].shape)
        drawn = base * np.exp(spread * noise) if base else spread * noise
        out[name] = jnp.asarray(drawn.astype(out[name].dtype))
    for name, factor in factors.items():
        out[name] = (out[name] * factor).astype(out[name].dtype)
    return out
```

```python
from contextlib import ExitStack

import concourse.bass as bass
from concourse import mybir

F32 = mybir.dt.float32
F32R = mybir.dt.float32r
BF16 = mybir.dt.bfloat16
I32 = mybir.dt.int32
ALU = mybir.AluOpType
ACT = mybir.ActivationFunctionType
AX = mybir.AxisListType

P = 128
GROUP = 4
UNROLL = 16
LOWEST = -3.0e38
EPS = 1e-5

LAG_X = 0
LAG_SCORE = 1
LAG_STEP = 2
LAG_COUNT = 3
LAG_CHECK = 7
LAG_PROB = 8
LAG_VALUE = 24
LAG_NORM1 = 25
LAG_YT = 26
LAG_HINGE = 30
LAG_OUT = 34
LAG_NORM2 = 35
LAG_FINAL = 36
FILL = 3


def build_kernel(nc, query, key_param, Wq, bq, Wk, bk, Wv, bv, Wo, bo,
                 Win, bin_, W1, b1, W2, b2, Wout, bout, out):
    B, L, D = query.shape
    S = key_param.shape[1]
    M, INNER = W1.shape
    HD = Wq.shape[1]
    E = 32
    H = HD // E
    C = D // P
    TILES = B * L // P
    KH = M * INNER // P
    HPC = P // S
    SCALE = 1.0 / float(E) ** 0.5
    TOP = 8
    assert D == HD == H * S == 512 and E == S == 32 and M * 2 == P and TILES % UNROLL == 0

    HALF = L // H
    assert 2 * HALF == P and L // H * H == L and TILES == B // 2 * UNROLL and H == UNROLL
    x_tiles = query.rearrange("(q b) (r j) d -> q j (b r) d", b=2, j=H)
    x_rows = query.rearrange("(q b) (h r) d -> q h b r d", b=2, h=H)
    out_rows = out.rearrange("(q b) (h r) d -> q h b r d", b=2, h=H)

    with ExitStack() as ctx:
        def sb(name, shape, dt=F32):
            return ctx.enter_context(nc.sbuf_tensor(name, shape, dt))

        def sem(name):
            return ctx.enter_context(nc.semaphore(name))

        XR, RR, YR, OR, UR, HR = 2, 2, 16, 2, 8, 2
        x_sb = sb("x_sb", [P, XR, D])
        xr_sb = sb("xr_sb", [P, RR, D])
        xT_hi = sb("xT_hi", [P, C, P], F32R)
        xT_lo = sb("xT_lo", [P, C, P], F32R)
        top8 = sb("top8", [P, H, TOP])
        cum = sb("cum", [P, H, TOP])
        tau = sb("tau", [P, H])
        u_sb = sb("u_sb", [P, UR // GROUP, H, GROUP, S])
        u_flat = u_sb[:].rearrange("p a h g s -> p (a h g s)")
        above = sb("above", [P, D])
        side = sb("side", [P, D], BF16)
        side2 = sb("side2", [P, D], BF16)
        count1 = sb("count1", [P, UR])
        count2 = sb("count2", [P, UR])
        sum_above = sb("sum_above", [P, H])
        sum_side = sb("sum_side", [P, H])
        twice = sb("twice", [P, H])
        twice_inv = sb("twice_inv", [P, H])
        step = sb("step", [P, H])
        differs = sb("differs", [P, GROUP])
        open_tiles = sb("open_tiles", [1, GROUP], I32)
        open_any = sb("open_any", [1, 1], I32)
        ones_col = sb("ones_col", [P, 1])
        pT = sb("pT", [P, 2 * H * C * P])
        oT_hi = sb("oT_hi", [P, C, P], F32R)
        oT_lo = sb("oT_lo", [P, C, P], F32R)
        r1 = sb("r1", [P, D])
        stats1 = sb("stats1", [P, 6])
        mv1 = sb("mv1", [P, 2, 2])
        ve1 = sb("ve1", [P, 1])
        rstd1 = sb("rstd1", [P, 2])
        shift1 = sb("shift1", [P, 2])
        y_sb = sb("y_sb", [P, YR, D])
        yT = sb("yT", [P, C, P])
        s_sb = sb("s_sb", [P, 2, GROUP * P])
        hinge = sb("hinge", [P, HR, GROUP * P])
        acc = sb("acc", [P, 2, GROUP * P])
        r2 = sb("r2", [P, D])
        stats2 = sb("stats2", [P, 6])
        mv2 = sb("mv2", [P, 2, 2])
        ve2 = sb("ve2", [P, 1])
        rstd2 = sb("rstd2", [P, 2])
        shift2 = sb("shift2", [P, 2])
        o_sb = sb("o_sb", [P, OR, D])
        A_hi = sb("A_hi", [P, C, D], F32R)
        A_lo = sb("A_lo", [P, C, D], F32R)
        Wo_hi = sb("Wo_hi", [P, C, D], F32R)
        Wo_lo = sb("Wo_lo", [P, C, D], F32R)
        V_blk = sb("V_blk", [P, H, P])
        bias_rows = sb("bias_rows", [P, D], F32R)
        pick_c = sb("pick_c", [P, P], F32R)
        pick_bo = sb("pick_bo", [P, P], F32R)
        WinD = sb("WinD", [P, C, 2, M])
        WoutD = sb("WoutD", [P, D])
        bout_bc = sb("bout_bc", [P, D])
        bin2 = sb("bin2", [P, 1])
        w1c = sb("w1c", [P, KH])
        b1c = sb("b1c", [P, KH])
        w2c = sb("w2c", [P, KH])
        b2c = sb("b2c", [P, 1])
        ident = sb("ident", [P, P])
        go_on = sb("go_on", [P, H, TOP])
        rank_inv = sb("rank_inv", [P, H, TOP])
        minus_half = sb("minus_half", [P, 1])
        eps = sb("eps", [P, 1])
        zero = sb("zero", [P, 1])
        minus_mean1 = sb("minus_mean1", [P, 1])
        minus_mean2 = sb("minus_mean2", [P, 1])
        z_col = cum[:].rearrange("p h k -> p (h k)").rearrange("p (r s) -> p r s", s=S)
        spare = top8[:].rearrange("p h k -> p (h k)")
        sorted_all, cum_all, cand_all = (spare[:, n * S:(n + 1) * S] for n in range(3))
        tau_one = sb("tau_one", [P, 1])
        ones_s = sb("ones_s", [P, S])
        rank_inv_all = sb("rank_inv_all", [P, S])
        Wk_sb, Wv_sb, Wq_sb, Wo_sb = (y_sb[:, n * C:(n + 1) * C, :] for n in range(4))
        A_f, WqT = (u_flat[:, n * C * D:(n + 1) * C * D].rearrange("p (c n) -> p c n", c=C) for n in range(2))
        kp_sb, c_full, bo_row, bv_row = (
            hinge[0:S, 0, :], hinge[0:1, 1, :], s_sb[0:1, 0, :], s_sb[0:1, 1, :])
        K_blk = acc[:, 0, :].rearrange("p (c n) -> p c n", c=C)
        bk_c = sb("bk_c", [P, C])
        bq_c = sb("bq_c", [P, C])
        ones_row = sb("ones_row", [1, P])
        kpT4, keysT4 = (r.rearrange("p (c n) -> p c n", c=C) for r in (acc[:, 1, :], r2[:]))

        banks = [ctx.enter_context(nc.psum_tensor(f"bank{i}", [P, 512], F32)) for i in range(8)]
        xT_ps, z_ps, uT_ps, v_ps, o_ps, ys_ps, f_ps = (
            banks[0], [banks[1], banks[2]], banks[3], banks[4], banks[5], banks[6], banks[7])

        s_x = [sem(f"s_x{i}") for i in range(XR)]
        s_store = [sem(f"s_store{i}") for i in range(OR)]
        s_xT, s_xhi, s_xlo = sem("s_xT"), sem("s_xhi"), sem("s_xlo")
        s_score, s_top, s_cum, s_cand, s_tau = sem("s_score"), sem("s_top"), sem("s_cum"), sem("s_cand"), sem("s_tau")
        s_u1, s_above, s_side, s_sums, s_sumc, s_twice, s_inv, s_step = (
            sem("s_u1"), sem("s_above"), sem("s_side"), sem("s_sums"), sem("s_sumc"), sem("s_twice"),
            sem("s_inv"), sem("s_step"))
        s_count2 = sem("s_count2")
        s_differs, s_opens, s_openr, s_checked = (
            sem("s_differs"), sem("s_opens"), sem("s_openr"), sem("s_checked"))
        s_u, s_uT, s_p, s_v, s_ohi, s_olo, s_o = (
            sem("s_u"), sem("s_uT"), sem("s_p"), sem("s_v"), sem("s_ohi"), sem("s_olo"), sem("s_o"))
        s_xr = [sem(f"s_xr{i}") for i in range(RR)]
        s_r1, s_st1, s_mv1, s_ve1, s_rstd1, s_shift1 = (
            sem("s_r1"), sem("s_st1"), sem("s_mv1"), sem("s_ve1"), sem("s_rstd1"), sem("s_shift1"))
        s_y, s_yb, s_yT, s_yTc, s_s = sem("s_y"), sem("s_yb"), sem("s_yT"), sem("s_yTc"), sem("s_s")
        s_sc = sem("s_sc")
        s_hinge, s_acc = sem("s_hinge"), sem("s_acc")
        s_f, s_r2, s_st2, s_mv2 = sem("s_f"), sem("s_r2"), sem("s_st2"), sem("s_mv2")
        s_ve2, s_rstd2, s_shift2, s_final = sem("s_ve2"), sem("s_rstd2"), sem("s_shift2"), sem("s_final")
        s_const, s_wload, s_smm, s_sev, s_ready = (
            sem("s_const"), sem("s_wload"), sem("s_smm"), sem("s_sev"), sem("s_ready"))
        s_neg1, s_neg2 = sem("s_neg1"), sem("s_neg2")
        s_zero, s_blk, s_c = sem("s_zero"), sem("s_blk"), sem("s_c")

        block = ctx.enter_context(nc.Block())
        SLOTS = TILES + FILL * UNROLL

        def slots(eng, slot, head=FILL, total=SLOTS):
            for turn in range(head):
                for j in range(UNROLL):
                    slot(turn, j)
            with eng.Fori(head, TILES // UNROLL) as turn:
                for j in range(UNROLL):
                    slot(turn, j)
            for turn in range(TILES // UNROLL, total // UNROLL):
                for j in range(UNROLL):
                    slot(turn, j)

        def in_range(turn, j, lag):
            return not isinstance(turn, int) or 0 <= turn * UNROLL + j - lag < TILES

        def pair_place(turn, i):
            pair = turn + i // UNROLL
            if isinstance(pair, int):
                return pair % 2 * (H * C * P)
            return pair % 2 * (H * C * P)

        def turns_of(turn, j, lag, ring):
            return turn * (UNROLL // ring) + (j - lag) // ring

        def batches(turn, j, half):
            lead = j - LAG_PROB
            if lead % GROUP < 2 and in_range(turn, j, LAG_PROB):
                yield lead - lead % GROUP, 2 * (lead % GROUP) + half

        def u_of(i):
            return u_sb[:, i // GROUP % 2, :, i % GROUP, :]

        def by_head(row):
            return row.rearrange("p (h s) -> p h s", h=H)

        def group_of(turn, i):
            return turn * (UNROLL // GROUP) + i // GROUP

        WLOADS = 23
        FILLS = 13 + TOP + S
        CONSTS = FILLS + 6

        @block.sync
        def _(sp):
            loads = [
                (kp_sb, key_param[0]),
                (Wk_sb, Wk.rearrange("(c p) n -> p c n", p=P)),
                (bk_c[:], bk.rearrange("(c p) -> p c", p=P)),
                (Wv_sb, Wv.rearrange("(c p) n -> p c n", p=P)),
                (bv_row, bv.rearrange("(a d) -> a d", a=1)),
                (Wq_sb, Wq.rearrange("(c p) n -> p c n", p=P)),
                (bq_c[:], bq.rearrange("(c p) -> p c", p=P)),
                (Wo_sb, Wo.rearrange("(c p) n -> p c n", p=P)),
                (bo_row, bo.rearrange("(a d) -> a d", a=1)),
                (WinD[:, :, 0, :], Win.rearrange("(c p) m -> p c m", p=P)),
                (WinD[:, :, 1, :], Win.rearrange("(c p) m -> p c m", p=P)),
                (bout_bc[:], bout.rearrange("(a d) -> a d", a=1).broadcast_to([P, D])),
                (b2c[0:M, :], b2.rearrange("(m a) -> m a", a=1)),
            ]
            for j in range(2):
                half = slice(j * M, (j + 1) * M)
                loads += [
                    (WoutD[half, :], Wout),
                    (bin2[half, :], bin_.rearrange("(m a) -> m a", a=1)),
                    (w1c[half, :], W1[:, j * KH:(j + 1) * KH]),
                    (b1c[half, :], b1[:, j * KH:(j + 1) * KH]),
                    (w2c[half, :], W2[:, j * KH:(j + 1) * KH]),
                ]
            sp.wait_ge(s_zero, 1)
            for dst, src in loads:
                sp.dma_start(dst, src, allow_slow_non_contiguous=True).then_inc(s_wload, 16)
            assert len(loads) == WLOADS

            LEAD = 1
            LAG_ROWS = LEAD + LAG_NORM1 - 1

            def slot(turn, j):
                base = turn * UNROLL
                if in_range(turn, j, 0):
                    tile = x_tiles[turn, j]
                    if not isinstance(turn, int) or base + j >= XR:
                        sp.wait_ge(s_xT, base + j - XR + 1)
                    sp.dma_start(x_sb[:, j % XR, :], tile).then_inc(s_x[j % XR], 16)
                if in_range(turn, j, LAG_ROWS):
                    i = j - LAG_ROWS
                    halves = [x_rows[turn + i // H, i % H, half] for half in range(2)]
                    if not isinstance(turn, int) or base + i >= RR:
                        sp.wait_ge(s_r1, base + i - RR + 1)
                    for half in range(2):
                        sp.dma_start(xr_sb[half * HALF:(half + 1) * HALF, i % RR, :], halves[half]).then_inc(s_xr[i % RR], 16)
                if in_range(turn, j, LEAD + LAG_FINAL + 1):
                    i = j - (LEAD + LAG_FINAL + 1)
                    halves = [out_rows[turn + i // H, i % H, half] for half in range(2)]
                    sp.wait_ge(s_final, base + i + 1)
                    for half in (1, 0):
                        sp.dma_start(halves[half], o_sb[half * HALF:(half + 1) * HALF, i % OR, :]).then_inc(
                                         s_store[i % OR], 16)

            slots(sp, slot)
            for r in range(OR):
                sp.wait_ge(s_store[r], 32 * (TILES // OR))

        @block.gpsimd
        def _(pool):
            nc.gpsimd.memset(b2c[:], 0.0).then_inc(s_zero, 1)
            nc.gpsimd.memset(ident[:], 0.0).then_inc(s_const, 1)
            nc.gpsimd.memset(go_on[:], 1.0).then_inc(s_const, 1)
            nc.gpsimd.memset(ones_s[:], 1.0).then_inc(s_const, 1)
            nc.gpsimd.memset(K_blk, 0.0).then_inc(s_const, 1)
            nc.gpsimd.memset(V_blk[:], 0.0).then_inc(s_const, 1)
            nc.gpsimd.memset(bias_rows[:].bitcast(F32), 0.0).then_inc(s_const, 1)
            nc.gpsimd.memset(pick_c[:].bitcast(F32), 0.0).then_inc(s_const, 1)
            nc.gpsimd.memset(pick_bo[:].bitcast(F32), 0.0).then_inc(s_const, 1)
            nc.gpsimd.memset(ones_row[:], 1.0).then_inc(s_const, 1)
            nc.gpsimd.memset(minus_half[:], -0.5).then_inc(s_const, 1)
            nc.gpsimd.memset(eps[:], EPS).then_inc(s_const, 1)
            nc.gpsimd.memset(zero[:], 0.0).then_inc(s_const, 1)
            for k in range(TOP):
                nc.gpsimd.memset(rank_inv[:, :, k:k + 1], 1.0 / (k + 1)).then_inc(s_const, 1)
            for k in range(S):
                nc.gpsimd.memset(rank_inv_all[:, k:k + 1], 1.0 / (k + 1)).then_inc(s_const, 1)
            nc.gpsimd.memset(ones_col[:], 1.0).then_inc(s_const, 1)
            pool.wait_ge(s_const, FILLS)
            nc.gpsimd.memset(go_on[:, :, 0:1], 0.0).then_inc(s_const, 1)
            for n, (pick, row) in enumerate(((pick_c, 0), (pick_c, E), (pick_bo, 2 * E), (pick_bo, 3 * E))):
                pool.wait_ge(s_const, FILLS + 1 + n)
                nc.gpsimd.memset(pick[row:row + 1, :].bitcast(F32), 1.0).then_inc(s_const, 1)
            pool.wait_ge(s_const, FILLS + 5)
            nc.gpsimd.affine_select(out=ident[:], in_=ident[:], compare_op=ALU.not_equal, fill=1.0,
                                    base=0, pattern=[[-1, P]], channel_multiplier=1).then_inc(s_const, 1)
            pool.wait_ge(s_wload, 16 * WLOADS)
            pool.wait_ge(s_const, CONSTS)

            def norm(t0, par, s_mv, mv, s_ve, ve, minus_mean, s_neg, s_rstd, rstd, s_shift, shift):
                if not isinstance(t0, int) or t0 >= 2:
                    pool.wait_ge(s_shift, t0 - 1)
                pool.wait_ge(s_mv, t0)
                nc.gpsimd.tensor_tensor(ve[:], mv[:, par, 1:2], eps[:], ALU.add).then_inc(s_ve, 1)
                nc.gpsimd.tensor_tensor(minus_mean[:], zero[:], mv[:, par, 0:1], ALU.subtract).then_inc(s_neg, 1)
                pool.wait_ge(s_ve, t0)
                nc.gpsimd.tensor_tensor(rstd[:, par:par + 1], ve[:], minus_half[:], ALU.pow).then_inc(s_rstd, 1)
                pool.wait_ge(s_rstd, t0)
                pool.wait_ge(s_neg, t0)
                nc.gpsimd.tensor_tensor(shift[:, par:par + 1], minus_mean[:], rstd[:, par:par + 1],
                                        ALU.mult).then_inc(s_shift, 1)

            def slot(turn, j):
                base = turn * UNROLL
                if in_range(turn, j, LAG_NORM1):
                    i = j - LAG_NORM1
                    norm(base + i + 1, i % 2, s_mv1, mv1, s_ve1, ve1, minus_mean1, s_neg1, s_rstd1, rstd1, s_shift1, shift1)
                if in_range(turn, j, LAG_NORM2):
                    i = j - LAG_NORM2
                    norm(base + i + 1, i % 2, s_mv2, mv2, s_ve2, ve2, minus_mean2, s_neg2, s_rstd2, rstd2, s_shift2, shift2)
                if in_range(turn, j, LAG_YT):
                    i = j - LAG_YT
                    pool.wait_ge(s_yT, base + i + 1)
                    nc.gpsimd.tensor_tensor(y_sb[:, i % YR, :], y_sb[:, i % YR, :], bout_bc[:],
                                            ALU.add).then_inc(s_yb, 1)

            slots(pool, slot)

        STEPS = ([("kpT", c) for c in range(C)] + [("keysT", c) for c in range(C)] + [("V", 0)]
                 + [("WqT", c) for c in range(C)] + [("c", 0)] + [("A", c) for c in range(C)])

        def done(name):
            return max(i for i, (n, _) in enumerate(STEPS) if n == name) + 1

        @block.tensor
        def _(pe):
            pe.wait_ge(s_wload, 16 * WLOADS)
            pe.wait_ge(s_const, CONSTS)
            for n, (name, c) in enumerate(STEPS):
                ps = banks[n % 8]
                if n >= 8:
                    pe.wait_ge(s_sev, n - 7)
                here = slice(c * P, (c + 1) * P)
                if name == "kpT":
                    mm = nc.tensor.transpose(ps[:, 0:S], kp_sb[:, here], ident[0:S, 0:S])
                elif name == "keysT":
                    if c == 0:
                        pe.wait_ge(s_sev, done("kpT"))
                    for d in range(C):
                        mm = nc.tensor.matmul(ps[:, 0:P], Wk_sb[:, d, here], kpT4[:, d, :],
                                              start=(d == 0), stop=(d == C - 1))
                elif name == "V":
                    pe.wait_ge(s_sev, done("keysT"))
                    for d in range(C):
                        nc.tensor.matmul(ps[:], keysT4[:, d, :], Wv_sb[:, d, :], start=(d == 0), stop=False)
                    mm = nc.tensor.matmul(ps[:], ones_row[:], bv_row, start=False, stop=True)
                elif name == "WqT":
                    for d in range(C):
                        mm = nc.tensor.transpose(ps[:, d * P:(d + 1) * P], Wq_sb[:, d, here], ident[:])
                elif name == "c":
                    pe.wait_ge(s_blk, C)
                    for k in range(C):
                        mm = nc.tensor.matmul(ps[0:1, k * P:(k + 1) * P], bq_c[:, k:k + 1], K_blk[:, k, :],
                                              start=True, stop=True)
                else:
                    if c == 0:
                        pe.wait_ge(s_sev, done("WqT"))
                    for k in range(C):
                        mm = nc.tensor.matmul(ps[:, k * P:(k + 1) * P], WqT[:, k, here], K_blk[:, k, :],
                                              start=True, stop=True)
                mm.then_inc(s_smm, 1)
            pe.wait_ge(s_ready, 4)
            pe.wait_ge(s_c, 4)
            pe.wait_ge(s_sev, len(STEPS))

            def three_pass(ps, hi, lo, w_hi, w_lo):
                for c in range(C):
                    nc.tensor.matmul(ps[:], hi[:, c, :], w_hi[:, c, :], start=False, stop=False)
                    nc.tensor.matmul(ps[:], hi[:, c, :], w_lo[:, c, :], start=False, stop=False)
                    mm = nc.tensor.matmul(ps[:], lo[:, c, :], w_hi[:, c, :], start=False, stop=(c == C - 1))
                return mm

            def probabilities(turn, j, half):
                for lead, b in batches(turn, j, half):
                    base = turn * UNROLL
                    if b == 0:
                        pe.wait_ge(s_checked, group_of(turn, lead) + 1)
                    if not isinstance(turn, int) or base + lead + b >= 1:
                        pe.wait_ge(s_p, base + lead + b)
                    for a in range(HPC):
                        mm = nc.tensor.transpose(
                            uT_ps[:, a * P:(a + 1) * P],
                            u_sb[:, lead // GROUP % 2, HPC * b + a].rearrange("p g s -> p (g s)"), ident[:])
                    mm.then_inc(s_uT, 1)

            def slot(turn, j):
                base = turn * UNROLL
                if in_range(turn, j, LAG_SCORE):
                    i = j - LAG_SCORE
                    pe.wait_ge(s_xhi, base + i + 1)
                    pe.wait_ge(s_xlo, base + i + 1)
                    if not isinstance(turn, int) or base + i >= 2:
                        pe.wait_ge(s_u1, base + i - 1)
                    z = z_ps[i % 2]
                    nc.tensor.matmul(z[:], pick_c[:], bias_rows[:], start=True, stop=False)
                    three_pass(z, xT_hi, xT_lo, A_hi, A_lo).then_inc(s_score, 1)
                probabilities(turn, j, 0)
                if in_range(turn, j, LAG_X):
                    i = j - LAG_X
                    pe.wait_ge(s_x[i % XR], 16 * (turns_of(turn, j, LAG_X, XR) + 1))
                    if not isinstance(turn, int) or base + i >= 1:
                        pe.wait_ge(s_xhi, base + i)
                        pe.wait_ge(s_xlo, base + i)
                    for c in range(C):
                        mm = nc.tensor.transpose(xT_ps[:, c * P:(c + 1) * P], x_sb[:, i % XR, c * P:(c + 1) * P],
                                                 ident[:])
                    mm.then_inc(s_xT, 1)
                if in_range(turn, j, LAG_VALUE):
                    i = j - LAG_VALUE
                    if i % UNROLL == 0:
                        pe.wait_ge(s_p, base + i + UNROLL)
                    if not isinstance(turn, int) or base + i >= 1:
                        pe.wait_ge(s_olo, base + i)
                    nc.tensor.matmul(v_ps[:], V_blk[:, i % H, :],
                                     pT[:, bass.ds(pair_place(turn, i) + i % H * C * P, C * P)],
                                     start=True, stop=True).then_inc(s_v, 1)
                probabilities(turn, j, 1)
                lead = j - LAG_CHECK
                if lead % GROUP == 0 and in_range(turn, j, LAG_CHECK):
                    pe.wait_ge(s_differs, group_of(turn, lead) + 1)
                    if not isinstance(turn, int) or base + lead > 0:
                        pe.wait_ge(s_p, base + lead)
                    nc.tensor.matmul(uT_ps[0:1, 0:GROUP], ones_col[:], differs[:], start=True,
                                     stop=True).then_inc(s_opens, 1)
                if in_range(turn, j, LAG_YT):
                    i = j - LAG_YT
                    pe.wait_ge(s_y, base + i + 1)
                    if not isinstance(turn, int) or base + i >= 1:
                        pe.wait_ge(s_sc, base + i)
                    for c in range(C):
                        mm = nc.tensor.transpose(ys_ps[:, c * P:(c + 1) * P], y_sb[:, i % YR, c * P:(c + 1) * P],
                                                 ident[:])
                    mm.then_inc(s_yT, 1)
                if in_range(turn, j, LAG_OUT):
                    i = j - LAG_OUT
                    if i % GROUP == 0:
                        pe.wait_ge(s_acc, (group_of(turn, i) + 1) * KH)
                    if not isinstance(turn, int) or base + i >= 1:
                        pe.wait_ge(s_r2, base + i)
                    q = i % GROUP
                    nc.tensor.matmul(f_ps[:], acc[:, (i // GROUP) % 2, q * P:(q + 1) * P], WoutD[:],
                                     start=True, stop=True).then_inc(s_f, 1)
                if in_range(turn, j, LAG_YT):
                    i = j - LAG_YT
                    pe.wait_ge(s_yTc, base + i + 1)
                    for c in range(C):
                        mm = nc.tensor.matmul(ys_ps[:, 0:P], WinD[:, c, :, :].rearrange("p a m -> p (a m)"),
                                              yT[:, c, :], start=(c == 0), stop=(c == C - 1))
                    mm.then_inc(s_s, 1)
                if in_range(turn, j, LAG_VALUE):
                    i = j - LAG_VALUE
                    pe.wait_ge(s_ohi, base + i + 1)
                    pe.wait_ge(s_olo, base + i + 1)
                    if not isinstance(turn, int) or base + i >= 1:
                        pe.wait_ge(s_r1, base + i)
                    nc.tensor.matmul(o_ps[:], pick_bo[:], bias_rows[:], start=True, stop=False)
                    three_pass(o_ps, oT_hi, oT_lo, Wo_hi, Wo_lo).then_inc(s_o, 1)

            slots(pe, slot)

        @block.scalar
        def _(act):
            for n, (name, c) in enumerate(STEPS):
                ps = banks[n % 8]
                act.wait_ge(s_smm, n + 1)
                if name == "kpT":
                    for a in range(HPC):
                        cp = nc.scalar.copy(kpT4[:, c, a * S:(a + 1) * S], ps[:, 0:S])
                    cp.then_inc(s_sev, 1)
                elif name == "keysT":
                    nc.scalar.activation(keysT4[:, c, :], ps[:, 0:P], ACT.Identity,
                                         bias=bk_c[:, c:c + 1]).then_inc(s_sev, 1)
                elif name == "V":
                    act.wait_ge(s_const, CONSTS)
                    for a in range(HPC):
                        rows = slice(a * S, (a + 1) * S)
                        cp = nc.scalar.copy(V_blk[rows, :, rows], ps[rows, :].rearrange("p (h d) -> p h d", h=H))
                    cp.then_inc(s_sev, 1)
                elif name == "WqT":
                    nc.scalar.copy(WqT[:, c, :], ps[:]).then_inc(s_sev, 1)
                elif name == "c":
                    nc.scalar.mul(c_full, ps[0:1, :], SCALE).then_inc(s_sev, 1)
                else:
                    nc.scalar.mul(A_f[:, c, :], ps[:], SCALE).then_inc(s_sev, 1)

            def probabilities(turn, j, half):
                for lead, b in batches(turn, j, half):
                    base = turn * UNROLL
                    jc, h0 = (lead // GROUP) % C, HPC * b
                    act.wait_ge(s_uT, base + lead + b + 1)
                    if not isinstance(turn, int) or base + lead >= 2 * UNROLL:
                        act.wait_ge(s_v, base + (lead - lead % UNROLL) - 2 * UNROLL + h0 + HPC)
                    place = pT[:, bass.ds(pair_place(turn, lead) + h0 * C * P, HPC * C * P)]
                    nc.scalar.activation(place.rearrange("p (a c n) -> p a c n", a=HPC, c=C)[:, :, jc, :],
                                         uT_ps[:].rearrange("p (a n) -> p a n", a=HPC),
                                         ACT.Relu).then_inc(s_p, 1)

            def slot(turn, j):
                base = turn * UNROLL
                if in_range(turn, j, LAG_STEP):
                    i = j - LAG_STEP
                    act.wait_ge(s_u1, base + i + 1)
                    if not isinstance(turn, int) or base + i >= 1:
                        act.wait_ge(s_sums, base + i)
                        act.wait_ge(s_sumc, base + i)
                    nc.scalar.activation(by_head(above[:]), u_of(i), ACT.Relu).then_inc(s_above, 1)
                    if (not isinstance(turn, int) or base + i >= UR) and i % GROUP == 0:
                        act.wait_ge(s_differs, group_of(turn, i) - 1)
                    nc.scalar.activation(by_head(side[:]), u_of(i), ACT.Sign,
                                         accum_out=count1[:, i % UR:i % UR + 1]).then_inc(s_side, 1)
                if in_range(turn, j, LAG_COUNT):
                    i = j - LAG_COUNT
                    act.wait_ge(s_u, base + i + 1)
                    if not isinstance(turn, int) or base + i >= 1:
                        act.wait_ge(s_count2, base + i)
                    nc.scalar.activation(by_head(side2[:]), u_of(i), ACT.Sign,
                                         accum_out=count2[:, i % UR:i % UR + 1]).then_inc(s_count2, 1)
                if in_range(turn, j, LAG_FINAL):
                    i = j - LAG_FINAL
                    act.wait_ge(s_shift2, base + i + 1)
                    act.wait_ge(s_r2, base + i + 1)
                    if not isinstance(turn, int) or base + i >= OR:
                        act.wait_ge(s_store[i % OR], 32 * turns_of(turn, j, LAG_FINAL, OR))
                    nc.scalar.activation(o_sb[:, i % OR, :], r2[:], ACT.Identity,
                                         bias=shift2[:, i % 2:i % 2 + 1], scale=rstd2[:, i % 2:i % 2 + 1]
                                         ).then_inc(s_final, 1)
                i = j - LAG_HINGE
                lead = i - i % GROUP
                if in_range(turn, 0, -lead):
                    g = group_of(turn, lead)
                    par = (lead // GROUP) % 2
                    if i % GROUP == 0:
                        act.wait_ge(s_sc, base + lead + GROUP)
                    for k in range(2 * (i % GROUP), 2 * (i % GROUP) + 2):
                        if not isinstance(turn, int) or base + lead > 0 or k >= HR:
                            act.wait_ge(s_acc, g * KH + k - HR + 1)
                        nc.scalar.activation(hinge[:, k % HR, :], s_sb[:, par, :], ACT.Relu,
                                             bias=b1c[:, k:k + 1], scale=w1c[:, k:k + 1]).then_inc(s_hinge, 1)
                probabilities(turn, j, 0)
                if in_range(turn, j, LAG_X):
                    i = j - LAG_X
                    act.wait_ge(s_xT, base + i + 1)
                    if not isinstance(turn, int) or base + i >= 1:
                        act.wait_ge(s_score, base + i)
                    nc.scalar.copy(xT_hi[:].rearrange("p c n -> p (c n)"), xT_ps[:]).then_inc(s_xhi, 1)
                if in_range(turn, j, LAG_VALUE):
                    i = j - LAG_VALUE
                    act.wait_ge(s_v, base + i + 1)
                    if not isinstance(turn, int) or base + i >= 1:
                        act.wait_ge(s_o, base + i)
                    nc.scalar.copy(oT_hi[:].rearrange("p c n -> p (c n)"), v_ps[:]).then_inc(s_ohi, 1)
                probabilities(turn, j, 1)
                if in_range(turn, j, LAG_YT):
                    i = j - LAG_YT
                    act.wait_ge(s_yT, base + i + 1)
                    if not isinstance(turn, int) or base + i >= 1:
                        act.wait_ge(s_s, base + i)
                    nc.scalar.copy(yT[:].rearrange("p c n -> p (c n)"), ys_ps[:]).then_inc(s_yTc, 1)
                if in_range(turn, j, LAG_NORM1):
                    i = j - LAG_NORM1
                    act.wait_ge(s_shift1, base + i + 1)
                    act.wait_ge(s_r1, base + i + 1)
                    if not isinstance(turn, int) or base + i >= YR:
                        act.wait_ge(s_r2, base + i - YR + 1)
                    nc.scalar.activation(y_sb[:, i % YR, :], r1[:], ACT.Identity,
                                         bias=shift1[:, i % 2:i % 2 + 1], scale=rstd1[:, i % 2:i % 2 + 1]
                                         ).then_inc(s_y, 1)
                if in_range(turn, j, LAG_YT):
                    i = j - LAG_YT
                    par, q = (i // GROUP) % 2, i % GROUP
                    act.wait_ge(s_s, base + i + 1)
                    if not isinstance(turn, int) or base + i >= 2 * GROUP:
                        act.wait_ge(s_hinge, (group_of(turn, i) - 1) * KH)
                    nc.scalar.activation(s_sb[:, par, q * P:(q + 1) * P], ys_ps[:, 0:P], ACT.Identity,
                                         bias=bin2[:]).then_inc(s_sc, 1)

            slots(act, slot)

        @block.vector
        def _(dve):
            dve.wait_ge(s_const, CONSTS)
            dve.wait_ge(s_sev, done("keysT"))
            for c in range(C):
                for a in range(HPC):
                    rows = slice(a * S, (a + 1) * S)
                    cp = nc.vector.tensor_copy(K_blk[rows, c, rows], keysT4[rows, c, 0:S])
                cp.then_inc(s_blk, 1)
            for n, (full, row, ready) in enumerate(((bo_row, 2 * E, 0), (c_full, 0, done("c")))):
                if ready:
                    dve.wait_ge(s_sev, ready)
                nc.vector.tensor_copy(bias_rows[row:row + 1, :], full).then_inc(s_c, 1)
                dve.wait_ge(s_c, 2 * n + 1)
                nc.vector.tensor_tensor(bias_rows[row + E:row + E + 1, :], full,
                                        bias_rows[row:row + 1, :].bitcast(F32), ALU.subtract).then_inc(s_c, 1)
            for n, (full, hi, lo, ready) in enumerate(((Wo_sb, Wo_hi, Wo_lo, 0), (A_f, A_hi, A_lo, done("A")))):
                if ready:
                    dve.wait_ge(s_sev, ready)
                nc.vector.tensor_copy(hi[:], full).then_inc(s_ready, 1)
                dve.wait_ge(s_ready, 2 * n + 1)
                nc.vector.tensor_tensor(lo[:], full, hi[:].bitcast(F32), ALU.subtract).then_inc(s_ready, 1)

            def spread(row):
                return row.unsqueeze(2).broadcast_to([P, H, S])

            def sort_tile(par, q):
                with dve.Fori(0, H) as h:
                    col = u_flat[:, bass.ds(h * (GROUP * S) + (par * H * GROUP + q) * S, S)]
                    nc.vector.tensor_copy(z_col[:, 0, :], col)
                    dve.drain()
                    for r in range(S // TOP):
                        eight = sorted_all[:, r * TOP:(r + 1) * TOP]
                        nc.vector.max(eight, z_col[:, r, :])
                        dve.drain()
                        if r < S // TOP - 1:
                            nc.vector.match_replace(z_col[:, r + 1, :], eight, z_col[:, r, :], LOWEST)
                            dve.drain()
                    nc.vector.tensor_tensor_scan(cum_all, ones_s[:], sorted_all, 0.0, ALU.mult, ALU.add)
                    dve.drain()
                    nc.vector.scalar_tensor_tensor(cand_all, cum_all, -1.0, rank_inv_all[:],
                                                   ALU.add, ALU.mult)
                    dve.drain()
                    nc.vector.tensor_reduce(tau_one[:], cand_all, AX.X, ALU.max)
                    dve.drain()
                    nc.vector.tensor_scalar(col, z_col[:, 0, :], tau_one[:], None, ALU.subtract)
                    dve.drain()

            def residual(t1, ps, s_prod, other, s_other, n_other, rows, s_rows, stats, s_st, s_used, s_before=None,
                         n_before=None):
                dve.wait_ge(s_prod, t1)
                dve.wait_ge(s_other, n_other)
                if not isinstance(t1, int) or t1 >= 2:
                    dve.wait_ge(s_used, t1 - 1)
                nc.vector.tensor_tensor(rows, ps[:], other, ALU.add).then_inc(s_rows, 1)
                if s_before is not None and not isinstance(t1, int):
                    dve.wait_ge(s_before, n_before)
                dve.wait_ge(s_rows, t1)
                nc.vector.bn_stats(stats[:], rows).then_inc(s_st, 1)

            def slot(turn, j):
                base = turn * UNROLL
                lead = j - LAG_CHECK
                checks = lead % GROUP == 0 and in_range(turn, j, LAG_CHECK)
                if checks:
                    g = group_of(turn, lead)
                    dve.wait_ge(s_count2, base + lead + GROUP)
                    places = slice(lead % UR, lead % UR + GROUP)
                    nc.vector.tensor_tensor(differs[:], count1[:, places], count2[:, places],
                                            ALU.not_equal).then_inc(s_differs, 1)
                if in_range(turn, j, LAG_NORM1):
                    i = j - LAG_NORM1
                    residual(base + i + 1, o_ps, s_o, xr_sb[:, i % RR, :], s_xr[i % RR],
                             32 * (turns_of(turn, j, LAG_NORM1, RR) + 1), r1[:], s_r1, stats1, s_st1, s_y)
                if in_range(turn, j, LAG_NORM2):
                    i = j - LAG_NORM2
                    residual(base + i + 1, f_ps, s_f, y_sb[:, i % YR, :], s_yb, base + i + 1, r2[:],
                             s_r2, stats2, s_st2, s_final, s_st1, base + (j - LAG_NORM1) + 1)
                if in_range(turn, j, LAG_NORM1):
                    i = j - LAG_NORM1
                    if isinstance(turn, int):
                        dve.wait_ge(s_st1, base + i + 1)
                    nc.vector.bn_aggr(mv1[:, i % 2, :], stats1[:]).then_inc(s_mv1, 1)
                if in_range(turn, j, LAG_STEP):
                    i = j - LAG_STEP
                    t1 = base + i + 1
                    if not isinstance(turn, int):
                        dve.wait_ge(s_st2, base + (j - LAG_NORM2) + 1)
                    dve.wait_ge(s_side, t1)
                    nc.vector.tensor_reduce(sum_side[:], by_head(side[:]), AX.X, ALU.add).then_inc(s_sumc, 1)
                if in_range(turn, j, LAG_NORM2):
                    i = j - LAG_NORM2
                    if isinstance(turn, int):
                        dve.wait_ge(s_st2, base + i + 1)
                    nc.vector.bn_aggr(mv2[:, i % 2, :], stats2[:]).then_inc(s_mv2, 1)
                if in_range(turn, j, LAG_STEP):
                    i = j - LAG_STEP
                    t1 = base + i + 1
                    dve.wait_ge(s_above, t1)
                    nc.vector.tensor_reduce(sum_above[:], by_head(above[:]), AX.X, ALU.add).then_inc(s_sums, 1)
                    dve.wait_ge(s_sumc, t1)
                    nc.vector.tensor_scalar(twice[:], sum_side[:], float(S), 2.0, ALU.add, ALU.max).then_inc(s_twice, 1)
                if in_range(turn, j, LAG_VALUE):
                    i = j - LAG_VALUE
                    dve.wait_ge(s_ohi, base + i + 1)
                    nc.vector.tensor_tensor(
                        oT_lo[:].rearrange("p c n -> p (c n)"), v_ps[:],
                        oT_hi[:].bitcast(F32).rearrange("p c n -> p (c n)"), ALU.subtract
                    ).then_inc(s_olo, 1)
                if in_range(turn, j, LAG_STEP):
                    i = j - LAG_STEP
                    t1 = base + i + 1
                    dve.wait_ge(s_twice, t1)
                    nc.vector.reciprocal(twice_inv[:], twice[:]).then_inc(s_inv, 1)
                if in_range(turn, j, LAG_X):
                    i = j - LAG_X
                    dve.wait_ge(s_xhi, base + i + 1)
                    nc.vector.tensor_tensor(
                        xT_lo[:].rearrange("p c n -> p (c n)"), xT_ps[:],
                        xT_hi[:].bitcast(F32).rearrange("p c n -> p (c n)"), ALU.subtract
                    ).then_inc(s_xlo, 1)
                if in_range(turn, j, LAG_STEP):
                    i = j - LAG_STEP
                    t1 = base + i + 1
                    if not isinstance(turn, int):
                        dve.wait_ge(s_score, base + (j - LAG_SCORE) + 1)
                    dve.wait_ge(s_inv, t1)
                    nc.vector.scalar_tensor_tensor(step[:], sum_above[:], -1.0, twice_inv[:], ALU.add,
                                                   ALU.mult).then_inc(s_step, 1)
                if in_range(turn, j, LAG_SCORE):
                    i = j - LAG_SCORE
                    if isinstance(turn, int):
                        dve.wait_ge(s_score, base + i + 1)
                    for h in range(H):
                        mx = nc.vector.max(top8[:, h, :], z_ps[i % 2][:, h * S:(h + 1) * S])
                    mx.then_inc(s_top, 1)
                if in_range(turn, j, LAG_STEP):
                    i = j - LAG_STEP
                    t1 = base + i + 1
                    dve.wait_ge(s_step, t1)
                    nc.vector.scalar_tensor_tensor(u_of(i), spread(step[:]), -2.0,
                                                   u_of(i), ALU.mult, ALU.add).then_inc(s_u, 1)
                if in_range(turn, j, LAG_SCORE):
                    i = j - LAG_SCORE
                    dve.wait_ge(s_top, base + i + 1)
                    nc.vector.tensor_tensor_scan(cum[:].rearrange("p h k -> p (h k)"),
                                                 go_on[:].rearrange("p h k -> p (h k)"),
                                                 top8[:].rearrange("p h k -> p (h k)"), 0.0,
                                                 ALU.mult, ALU.add).then_inc(s_cum, 1)
                hinge_step(turn, j, 0)
                if in_range(turn, j, LAG_SCORE):
                    i = j - LAG_SCORE
                    dve.wait_ge(s_cum, base + i + 1)
                    nc.vector.scalar_tensor_tensor(cum[:], cum[:], -1.0, rank_inv[:], ALU.add,
                                                   ALU.mult).then_inc(s_cand, 1)
                hinge_step(turn, j, 1)
                if in_range(turn, j, LAG_SCORE):
                    i = j - LAG_SCORE
                    dve.wait_ge(s_cand, base + i + 1)
                    nc.vector.tensor_reduce(tau[:], cum[:], AX.X, ALU.max).then_inc(s_tau, 1)
                    dve.wait_ge(s_tau, base + i + 1)
                    if not isinstance(base, int) or base + i >= UR:
                        dve.wait_ge(s_uT, base + (i - i % GROUP) - UR + GROUP)
                    nc.vector.tensor_tensor(u_of(i), by_head(z_ps[i % 2][:]),
                                            spread(tau[:]), ALU.subtract).then_inc(s_u1, 1)
                if checks:
                    g = group_of(turn, lead)
                    dve.wait_ge(s_opens, g + 1)
                    nc.vector.tensor_copy(open_tiles[:], uT_ps[0:1, 0:GROUP]).then_inc(s_openr, 1)
                    nc.vector.tensor_reduce(open_any[:], uT_ps[0:1, 0:GROUP], AX.X, ALU.max).then_inc(s_openr, 1)
                    dve.drain()
                    with dve.If(dve.value_load(open_any[:], min_val=0, max_val=P) > 0):
                        for q in range(GROUP):
                            with dve.If(dve.value_load(open_tiles[:, q:q + 1], min_val=0, max_val=P) > 0):
                                sort_tile(lead // GROUP % 2, q)
                    dve.nop().then_inc(s_checked, 1)

            def hinge_step(turn, j, half):
                base = turn * UNROLL
                i = j - LAG_HINGE
                first = i - i % GROUP
                if not in_range(turn, 0, -first):
                    return
                g, par, k = group_of(turn, first), (first // GROUP) % 2, 2 * (i % GROUP) + half
                dve.wait_ge(s_hinge, g * KH + k + 1)
                if k == 0:
                    if not isinstance(base, int) or base + first >= 2 * GROUP:
                        dve.wait_ge(s_f, base + first - GROUP)
                    nc.vector.tensor_scalar(acc[:, par, :], hinge[:, k % HR, :], w2c[:, k:k + 1], b2c[:],
                                            ALU.mult, ALU.add).then_inc(s_acc, 1)
                else:
                    dve.wait_ge(s_acc, g * KH + k)
                    nc.vector.scalar_tensor_tensor(acc[:, par, :], hinge[:, k % HR, :], w2c[:, k:k + 1],
                                                   acc[:, par, :], ALU.mult, ALU.add).then_inc(s_acc, 1)

            slots(dve, slot)


_INS = ['query', 'key_param', 'Wq', 'bq', 'Wk', 'bk', 'Wv', 'bv', 'Wo', 'bo']
_FFN = ['Win', 'bin_', 'W1', 'b1', 'W2', 'b2', 'Wout', 'bout']
_NAMES = ['L0_attn_' + n for n in _INS] + ['L0_ffn_' + n for n in _FFN]
_OUTS = [((16, 1024, 512), 'float32')]


def kernel(**inputs):
    import numpy as _np
    import concourse.bacc as _bacc
    from concourse import mybir as _mybir
    from concourse.bass_utils import run_bass_kernel_spmd as _run

    nc = _bacc.Bacc("TRN2", target_bir_lowering=False, num_devices=1)
    arrays, args = {}, []
    for name in _NAMES:
        a = _np.ascontiguousarray(inputs[name])
        arrays[f"in_{name}_dram"] = a
        args.append(nc.dram_tensor(f"in_{name}_dram", a.shape, _mybir.dt.from_np(a.dtype), kind="ExternalInput").ap())
    for i, (shape, dtype) in enumerate(_OUTS):
        dt = _mybir.dt.from_np(_np.dtype(dtype))
        args.append(nc.dram_tensor(f"out_{i}_dram", shape, dt, kind="ExternalOutput").ap())
    build_kernel(nc, *args)
    r = _run(nc, [arrays], core_ids=[0])
    got = tuple(r.results[0][f"out_{i}_dram"] for i in range(len(_OUTS)))
    return got[0]
```

```python
from contextlib import ExitStack

import concourse.bass as bass
from concourse import mybir

F32 = mybir.dt.float32
F32R = mybir.dt.float32r
BF16 = mybir.dt.bfloat16
I32 = mybir.dt.int32
ALU = mybir.AluOpType
ACT = mybir.ActivationFunctionType
AX = mybir.AxisListType

P = 128
GROUP = 4
UNROLL = 16
LOWEST = -3.0e38
EPS = 1e-5

LAG_X = 0
LAG_SCORE = 1
LAG_SIDE = 2
LAG_STEP = 3
LAG_COUNT = 4
LAG_CHECK = 8
LAG_PROB = 9
LAG_XB = 25
LAG_VALUE = 24
LAG_WO = 25
LAG_NORM1 = 26
LAG_Y = 27
LAG_YT = 28
LAG_S = 29
LAG_SC = 30
LAG_HINGE = 33
LAG_OUT = 37
LAG_NORM2 = 38
LAG_FINAL = 39
FILL = 3


def build_kernel(nc, query, key_param, Wq, bq, Wk, bk, Wv, bv, Wo, bo,
                 Win, bin_, W1, b1, W2, b2, Wout, bout, out):
    B, L, D = query.shape
    S = key_param.shape[1]
    M, INNER = W1.shape
    HD = Wq.shape[1]
    E = 32
    H = HD // E
    C = D // P
    TILES = B * L // P
    KH = M * INNER // P
    HPC = P // S
    SCALE = 1.0 / float(E) ** 0.5
    TOP = 8
    assert D == HD == H * S == 512 and E == S == 32 and M * 2 == P and TILES % UNROLL == 0

    HALF = L // H
    assert 2 * HALF == P and L // H * H == L and TILES == B // 2 * UNROLL and H == UNROLL
    x_tiles = query.rearrange("(q b) (r j) d -> q j (b r) d", b=2, j=H)
    x_rows = query.rearrange("(q b) (h r) d -> q h b r d", b=2, h=H)
    out_rows = out.rearrange("(q b) (h r) d -> q h b r d", b=2, h=H)

    with ExitStack() as ctx:
        def sb(name, shape, dt=F32):
            return ctx.enter_context(nc.sbuf_tensor(name, shape, dt))

        def sem(name):
            return ctx.enter_context(nc.semaphore(name))

        XR, RR, YR, OR, UR, HR = 2, 2, 16, 2, 8, 2
        x_sb = sb("x_sb", [P, XR, D])
        xr_sb = sb("xr_sb", [P, RR, D])
        xT_hi = sb("xT_hi", [P, C, P], F32R)
        xT_lo = sb("xT_lo", [P, C, P], F32R)
        top8 = sb("top8", [P, H, TOP])
        cum = sb("cum", [P, H, TOP])
        tau = sb("tau", [P, H])
        u_sb = sb("u_sb", [P, UR // GROUP, H, GROUP, S])
        u_raw = sb("u_raw", [P, 2, D])
        u_flat = u_sb[:].rearrange("p a h g s -> p (a h g s)")
        above = sb("above", [P, D])
        side = sb("side", [P, D], BF16)
        unread = sb("unread", [P, D], BF16)
        count1 = sb("count1", [P, UR])
        count2 = sb("count2", [P, UR])
        sum_above = sb("sum_above", [P, H])
        sum_side = sb("sum_side", [P, H])
        twice = sb("twice", [P, H])
        twice_inv = sb("twice_inv", [P, H])
        step = sb("step", [P, H])
        differs = sb("differs", [P, GROUP])
        open_tiles = sb("open_tiles", [1, GROUP], I32)
        open_any = sb("open_any", [1, 1], I32)
        ones_col = sb("ones_col", [P, 1])
        pT = sb("pT", [P, 2 * H * C * P])
        oT_hi = sb("oT_hi", [P, C, P], F32R)
        oT_lo = sb("oT_lo", [P, C, P], F32R)
        sum1 = sb("sum1", [P, 2])
        minus_mean1 = sb("minus_mean1", [P, 2])
        shift_sq1 = sb("shift_sq1", [P, 2])
        var1 = sb("var1", [P, 2])
        ve1 = sb("ve1", [P, 1])
        rstd1 = sb("rstd1", [P, 2])
        shift1 = sb("shift1", [P, 2])
        y_sb = sb("y_sb", [P, YR, D])
        yT = sb("yT", [P, C, P])
        s_sb = sb("s_sb", [P, 2, GROUP * P])
        hinge = sb("hinge", [P, HR, GROUP * P])
        acc = sb("acc", [P, 2, GROUP * P])
        sum2 = sb("sum2", [P, 2])
        minus_mean2 = sb("minus_mean2", [P, 2])
        shift_sq2 = sb("shift_sq2", [P, 2])
        var2 = sb("var2", [P, 2])
        ve2 = sb("ve2", [P, 1])
        rstd2 = sb("rstd2", [P, 2])
        shift2 = sb("shift2", [P, 2])
        o_sb = sb("o_sb", [P, OR, D])
        A_hi = sb("A_hi", [P, C, D], F32R)
        A_lo = sb("A_lo", [P, C, D], F32R)
        Wo_hi = sb("Wo_hi", [P, C, D], F32R)
        Wo_lo = sb("Wo_lo", [P, C, D], F32R)
        V_blk = sb("V_blk", [P, H, P])
        bias_rows = sb("bias_rows", [P, D], F32R)
        pick_c = sb("pick_c", [P, P], F32R)
        bo_bc = sb("bo_bc", [P, D])
        Win_sb = sb("Win_sb", [P, C, M])
        s_rows = sb("s_rows", [P, 2, M])
        WoutD = sb("WoutD", [P, D])
        bout_bc = sb("bout_bc", [P, D])
        bin2 = sb("bin2", [P, 1])
        w1c = sb("w1c", [P, KH])
        b1c = sb("b1c", [P, KH])
        w2c = sb("w2c", [P, KH])
        b2c = sb("b2c", [P, 1])
        ident = sb("ident", [P, P])
        go_on = sb("go_on", [P, H, TOP])
        rank_inv = sb("rank_inv", [P, S])
        minus_half = sb("minus_half", [P, 1])
        eps = sb("eps", [P, 1])
        per_row = sb("per_row", [P, 1])
        per_row_sq = sb("per_row_sq", [P, 1])
        rest = cum[:].rearrange("p h k -> p (h k)").rearrange("p (a s) -> p a s", s=S)
        ranked = top8[:].rearrange("p h k -> p (h k)").rearrange("p (a s) -> p a s", s=S)
        ones_s = sb("ones_s", [P, S])
        tau_some = sb("tau_some", [P, HPC])
        Wk_sb, Wv_sb, Wq_sb, Wo_sb = (y_sb[:, n * C:(n + 1) * C, :] for n in range(4))
        A_f, WqT = (u_flat[:, n * C * D:(n + 1) * C * D].rearrange("p (c n) -> p c n", c=C) for n in range(2))
        kp_sb, c_full, bv_row = (
            hinge[0:S, 0, :], hinge[0:1, 1, :], s_sb[0:1, 1, :])
        K_blk = acc[:, 0, :].rearrange("p (c n) -> p c n", c=C)
        bk_c = sb("bk_c", [P, C])
        bq_c = sb("bq_c", [P, C])
        ones_row = above[0:1, 0:P]
        kpT4, keysT4 = (r.rearrange("p (c n) -> p c n", c=C) for r in (acc[:, 1, :], o_sb[:, 0, :]))

        banks = [ctx.enter_context(nc.psum_tensor(f"bank{i}", [P, 512], F32)) for i in range(8)]
        xT_ps, z_ps, uT_ps, v_ps, o_ps, ys_ps, f_ps = (
            banks[0], [banks[1], banks[2]], banks[3], banks[4], banks[5], banks[6], banks[7])

        s_x = [sem(f"s_x{i}") for i in range(XR)]
        s_store = [sem(f"s_store{i}") for i in range(OR)]
        s_xT, s_xhi, s_xlo = sem("s_xT"), sem("s_xhi"), sem("s_xlo")
        s_score, s_top, s_cum, s_cand, s_tau = sem("s_score"), sem("s_top"), sem("s_cum"), sem("s_cand"), sem("s_tau")
        s_u1, s_above, s_side, s_sums, s_sumc, s_twice, s_inv, s_step = (
            sem("s_u1"), sem("s_above"), sem("s_side"), sem("s_sums"), sem("s_sumc"), sem("s_twice"),
            sem("s_inv"), sem("s_step"))
        s_count2 = sem("s_count2")
        s_differs, s_opens, s_openr, s_checked = (
            sem("s_differs"), sem("s_opens"), sem("s_openr"), sem("s_checked"))
        s_u, s_uT, s_p, s_v, s_ohi, s_olo, s_o = (
            sem("s_u"), sem("s_uT"), sem("s_p"), sem("s_v"), sem("s_ohi"), sem("s_olo"), sem("s_o"))
        s_xr = [sem(f"s_xr{i}") for i in range(RR)]
        s_r1, s_mean1, s_var1, s_ve1, s_rstd1, s_shift1 = (
            sem("s_r1"), sem("s_mean1"), sem("s_var1"), sem("s_ve1"), sem("s_rstd1"), sem("s_shift1"))
        s_xb = sem("s_xb")
        s_y, s_yb, s_yT, s_yTc, s_s = sem("s_y"), sem("s_yb"), sem("s_yT"), sem("s_yTc"), sem("s_s")
        s_srow, s_sT, s_sc = sem("s_srow"), sem("s_sT"), sem("s_sc")
        s_hinge, s_acc = sem("s_hinge"), sem("s_acc")
        s_f, s_r2, s_mean2, s_var2 = sem("s_f"), sem("s_r2"), sem("s_mean2"), sem("s_var2")
        s_foldc, s_folds = sem("s_foldc"), sem("s_folds")
        s_ve2, s_rstd2, s_shift2, s_final = sem("s_ve2"), sem("s_rstd2"), sem("s_shift2"), sem("s_final")
        s_const, s_wload, s_smm, s_sev, s_ready = (
            sem("s_const"), sem("s_wload"), sem("s_smm"), sem("s_sev"), sem("s_ready"))
        s_zero, s_blk, s_c = sem("s_zero"), sem("s_blk"), sem("s_c")

        block = ctx.enter_context(nc.Block())
        SLOTS = TILES + FILL * UNROLL

        def slots(eng, slot, head=FILL, total=SLOTS):
            for turn in range(head):
                for j in range(UNROLL):
                    slot(turn, j)
            with eng.Fori(head, TILES // UNROLL) as turn:
                for j in range(UNROLL):
                    slot(turn, j)
            for turn in range(TILES // UNROLL, total // UNROLL):
                for j in range(UNROLL):
                    slot(turn, j)

        def in_range(turn, j, lag):
            return not isinstance(turn, int) or 0 <= turn * UNROLL + j - lag < TILES

        def so_far(turn, j, lag):
            n = turn * UNROLL + j - lag + 1
            return min(max(n, 0), TILES) if isinstance(n, int) else n

        def pair_place(turn, i):
            return (turn + i // UNROLL) % 2 * (H * C * P)

        def turns_of(turn, j, lag, ring):
            return turn * (UNROLL // ring) + (j - lag) // ring

        def batches(turn, j, half):
            lead = j - LAG_PROB
            if lead % GROUP < 2 and in_range(turn, j, LAG_PROB):
                yield lead - lead % GROUP, 2 * (lead % GROUP) + half

        def u_of(i):
            return u_sb[:, i // GROUP % 2, :, i % GROUP, :]

        def by_head(row):
            return row.rearrange("p (h s) -> p h s", h=H)

        def group_of(turn, i):
            return turn * (UNROLL // GROUP) + i // GROUP

        WLOADS = 22
        FILLS = 13 + S
        CONSTS = FILLS + 4

        @block.sync
        def _(sp):
            loads = [
                (kp_sb, key_param[0]),
                (Wk_sb, Wk.rearrange("(c p) n -> p c n", p=P)),
                (bk_c[:], bk.rearrange("(c p) -> p c", p=P)),
                (Wv_sb, Wv.rearrange("(c p) n -> p c n", p=P)),
                (bv_row, bv.rearrange("(a d) -> a d", a=1)),
                (Wq_sb, Wq.rearrange("(c p) n -> p c n", p=P)),
                (bq_c[:], bq.rearrange("(c p) -> p c", p=P)),
                (Wo_sb, Wo.rearrange("(c p) n -> p c n", p=P)),
                (bo_bc[:], bo.rearrange("(a d) -> a d", a=1).broadcast_to([P, D])),
                (Win_sb[:], Win.rearrange("(c p) m -> p c m", p=P)),
                (bout_bc[:], bout.rearrange("(a d) -> a d", a=1).broadcast_to([P, D])),
                (b2c[0:M, :], b2.rearrange("(m a) -> m a", a=1)),
            ]
            for j in range(2):
                half = slice(j * M, (j + 1) * M)
                loads += [
                    (WoutD[half, :], Wout),
                    (bin2[half, :], bin_.rearrange("(m a) -> m a", a=1)),
                    (w1c[half, :], W1[:, j * KH:(j + 1) * KH]),
                    (b1c[half, :], b1[:, j * KH:(j + 1) * KH]),
                    (w2c[half, :], W2[:, j * KH:(j + 1) * KH]),
                ]
            sp.wait_ge(s_zero, 1)
            for dst, src in loads:
                sp.dma_start(dst, src, allow_slow_non_contiguous=True).then_inc(s_wload, 16)
            assert len(loads) == WLOADS

            LAG_STORE = LAG_FINAL + 2

            def slot(turn, j):
                base = turn * UNROLL
                if in_range(turn, j, 0):
                    tile = x_tiles[turn, j]
                    if not isinstance(turn, int) or base + j >= XR:
                        sp.wait_ge(s_xT, base + j - XR + 1)
                    sp.dma_start(x_sb[:, j % XR, :], tile).then_inc(s_x[j % XR], 16)
                if in_range(turn, j, LAG_NORM1):
                    i = j - LAG_NORM1
                    halves = [x_rows[turn + i // H, i % H, half] for half in range(2)]
                    if not isinstance(turn, int) or base + i >= RR:
                        sp.wait_ge(s_r1, base + i - RR + 1)
                    for half in range(2):
                        sp.dma_start(xr_sb[half * HALF:(half + 1) * HALF, i % RR, :], halves[half]).then_inc(s_xr[i % RR], 16)
                if in_range(turn, j, LAG_STORE):
                    i = j - LAG_STORE
                    halves = [out_rows[turn + i // H, i % H, half] for half in range(2)]
                    sp.wait_ge(s_final, base + i + 1)
                    for half in (1, 0):
                        sp.dma_start(halves[half], o_sb[half * HALF:(half + 1) * HALF, i % OR, :]).then_inc(
                                         s_store[i % OR], 16)

            slots(sp, slot)
            for r in range(OR):
                sp.wait_ge(s_store[r], 32 * (TILES // OR))

        @block.gpsimd
        def _(pool):
            nc.gpsimd.memset(b2c[:], 0.0).then_inc(s_zero, 1)
            nc.gpsimd.memset(ident[:], 0.0).then_inc(s_const, 1)
            nc.gpsimd.memset(go_on[:], 1.0).then_inc(s_const, 1)
            nc.gpsimd.memset(ones_s[:], 1.0).then_inc(s_const, 1)
            nc.gpsimd.memset(K_blk, 0.0).then_inc(s_const, 1)
            nc.gpsimd.memset(V_blk[:], 0.0).then_inc(s_const, 1)
            nc.gpsimd.memset(bias_rows[:].bitcast(F32), 0.0).then_inc(s_const, 1)
            nc.gpsimd.memset(pick_c[:].bitcast(F32), 0.0).then_inc(s_const, 1)
            nc.gpsimd.memset(ones_row, 1.0).then_inc(s_const, 1)
            nc.gpsimd.memset(minus_half[:], -0.5).then_inc(s_const, 1)
            nc.gpsimd.memset(eps[:], EPS).then_inc(s_const, 1)
            nc.gpsimd.memset(per_row[:], -1.0 / D).then_inc(s_const, 1)
            nc.gpsimd.memset(per_row_sq[:], -1.0 / D ** 1.5).then_inc(s_const, 1)
            for k in range(S):
                nc.gpsimd.memset(rank_inv[:, k:k + 1], 1.0 / (k + 1)).then_inc(s_const, 1)
            nc.gpsimd.memset(ones_col[:], 1.0).then_inc(s_const, 1)
            pool.wait_ge(s_const, FILLS)
            nc.gpsimd.memset(go_on[:, :, 0:1], 0.0).then_inc(s_const, 1)
            for n, row in enumerate((0, E)):
                pool.wait_ge(s_const, FILLS + 1 + n)
                nc.gpsimd.memset(pick_c[row:row + 1, :].bitcast(F32), 1.0).then_inc(s_const, 1)
            pool.wait_ge(s_const, FILLS + 3)
            nc.gpsimd.affine_select(out=ident[:], in_=ident[:], compare_op=ALU.not_equal, fill=1.0,
                                    base=0, pattern=[[-1, P]], channel_multiplier=1).then_inc(s_const, 1)
            pool.wait_ge(s_wload, 16 * WLOADS)
            pool.wait_ge(s_const, CONSTS)

            def mean(t0, par, s_rows, total, s_mean, minus_mean, shift_sq, s_shift):
                if not isinstance(t0, int) or t0 >= 3:
                    pool.wait_ge(s_shift, t0 - 2)
                pool.wait_ge(s_rows, t0)
                nc.gpsimd.tensor_tensor(shift_sq[:, par:par + 1], total[:, par:par + 1], per_row_sq[:],
                                        ALU.mult).then_inc(s_mean, 1)
                nc.gpsimd.tensor_tensor(minus_mean[:, par:par + 1], total[:, par:par + 1], per_row[:],
                                        ALU.mult).then_inc(s_mean, 1)

            def norm(t0, par, s_var, var, s_ve, ve, s_mean, minus_mean, s_rstd, rstd, s_shift, shift, s_used):
                if not isinstance(t0, int) or t0 >= 2:
                    pool.wait_ge(s_rstd, t0 - 1)
                pool.wait_ge(s_var, t0)
                nc.gpsimd.tensor_tensor(ve[:], var[:, par:par + 1], eps[:], ALU.add).then_inc(s_ve, 1)
                if not isinstance(t0, int) or t0 >= 3:
                    pool.wait_ge(s_used, t0 - 2)
                    pool.wait_ge(s_shift, t0 - 2)
                pool.wait_ge(s_ve, t0)
                nc.gpsimd.tensor_tensor(rstd[:, par:par + 1], ve[:], minus_half[:], ALU.pow).then_inc(s_rstd, 1)
                pool.wait_ge(s_mean, 2 * t0)
                pool.wait_ge(s_rstd, t0)
                nc.gpsimd.tensor_tensor(shift[:, par:par + 1], minus_mean[:, par:par + 1], rstd[:, par:par + 1],
                                        ALU.mult).then_inc(s_shift, 1)

            def fold(s_in, t1, row, s_out):
                halves = by_head(row[:]).rearrange("p h (a s) -> p h a s", a=2)
                pool.wait_ge(s_in, t1)
                nc.gpsimd.tensor_tensor(halves[:, :, 0, :], halves[:, :, 0, :], halves[:, :, 1, :],
                                        ALU.add).then_inc(s_out, 1)

            def slot(turn, j):
                base = turn * UNROLL
                if in_range(turn, j, LAG_Y):
                    i = j - LAG_Y
                    norm(base + i + 1, i % 2, s_var1, var1, s_ve1, ve1, s_mean1, minus_mean1, s_rstd1, rstd1,
                         s_shift1, shift1, s_y)
                if in_range(turn, j, LAG_FINAL):
                    i = j - LAG_FINAL
                    norm(base + i + 1, i % 2, s_var2, var2, s_ve2, ve2, s_mean2, minus_mean2, s_rstd2, rstd2,
                         s_shift2, shift2, s_final)
                if in_range(turn, j, LAG_NORM1):
                    i = j - LAG_NORM1
                    mean(base + i + 1, i % 2, s_r1, sum1, s_mean1, minus_mean1, shift_sq1, s_shift1)
                if in_range(turn, j, LAG_NORM2):
                    i = j - LAG_NORM2
                    mean(base + i + 1, i % 2, s_r2, sum2, s_mean2, minus_mean2, shift_sq2, s_shift2)
                if in_range(turn, j, LAG_XB):
                    i = j - LAG_XB
                    pool.wait_ge(s_xr[i % RR], 32 * (turns_of(turn, j, LAG_XB, RR) + 1))
                    nc.gpsimd.tensor_tensor(xr_sb[:, i % RR, :], xr_sb[:, i % RR, :], bo_bc[:],
                                            ALU.add).then_inc(s_xb, 1)
                if in_range(turn, j, LAG_YT):
                    i = j - LAG_YT
                    pool.wait_ge(s_yT, base + i + 1)
                    nc.gpsimd.tensor_tensor(y_sb[:, i % YR, :], y_sb[:, i % YR, :], bout_bc[:],
                                            ALU.add).then_inc(s_yb, 1)
                if in_range(turn, j, LAG_SIDE):
                    i = j - LAG_SIDE
                    fold(s_side, base + i + 1, side, s_foldc)
                    fold(s_above, base + i + 1, above, s_folds)

            slots(pool, slot)

        STEPS = ([("kpT", c) for c in range(C)] + [("keysT", c) for c in range(C)] + [("V", 0)]
                 + [("WqT", c) for c in range(C)] + [("c", 0)] + [("A", c) for c in range(C)])

        def done(name):
            return max(i for i, (n, _) in enumerate(STEPS) if n == name) + 1

        @block.tensor
        def _(pe):
            pe.wait_ge(s_wload, 16 * WLOADS)
            pe.wait_ge(s_const, CONSTS)
            for n, (name, c) in enumerate(STEPS):
                ps = banks[n % 8]
                if n >= 8:
                    pe.wait_ge(s_sev, n - 7)
                here = slice(c * P, (c + 1) * P)
                if name == "kpT":
                    mm = nc.tensor.transpose(ps[:, 0:S], kp_sb[:, here], ident[0:S, 0:S])
                elif name == "keysT":
                    if c == 0:
                        pe.wait_ge(s_sev, done("kpT"))
                    for d in range(C):
                        mm = nc.tensor.matmul(ps[:, 0:P], Wk_sb[:, d, here], kpT4[:, d, :],
                                              start=(d == 0), stop=(d == C - 1))
                elif name == "V":
                    pe.wait_ge(s_sev, done("keysT"))
                    for d in range(C):
                        nc.tensor.matmul(ps[:], keysT4[:, d, :], Wv_sb[:, d, :], start=(d == 0), stop=False)
                    mm = nc.tensor.matmul(ps[:], ones_row, bv_row, start=False, stop=True)
                elif name == "WqT":
                    for d in range(C):
                        mm = nc.tensor.transpose(ps[:, d * P:(d + 1) * P], Wq_sb[:, d, here], ident[:])
                elif name == "c":
                    pe.wait_ge(s_blk, C)
                    for k in range(C):
                        mm = nc.tensor.matmul(ps[0:1, k * P:(k + 1) * P], bq_c[:, k:k + 1], K_blk[:, k, :],
                                              start=True, stop=True)
                else:
                    if c == 0:
                        pe.wait_ge(s_sev, done("WqT"))
                    for k in range(C):
                        mm = nc.tensor.matmul(ps[:, k * P:(k + 1) * P], WqT[:, k, here], K_blk[:, k, :],
                                              start=True, stop=True)
                mm.then_inc(s_smm, 1)
            pe.wait_ge(s_ready, 4)
            pe.wait_ge(s_c, 2)
            pe.wait_ge(s_sev, len(STEPS))

            def three_pass(ps, hi, lo, w_hi, w_lo, start):
                for c in range(C):
                    nc.tensor.matmul(ps[:], hi[:, c, :], w_hi[:, c, :], start=start and c == 0, stop=False)
                    nc.tensor.matmul(ps[:], hi[:, c, :], w_lo[:, c, :], start=False, stop=False)
                    mm = nc.tensor.matmul(ps[:], lo[:, c, :], w_hi[:, c, :], start=False, stop=(c == C - 1))
                return mm

            def probabilities(turn, j, half):
                for lead, b in batches(turn, j, half):
                    base = turn * UNROLL
                    if b == 0:
                        pe.wait_ge(s_checked, group_of(turn, lead) + 1)
                    if not isinstance(turn, int) or base + lead + b >= 1:
                        pe.wait_ge(s_p, base + lead + b)
                    for a in range(HPC):
                        mm = nc.tensor.transpose(
                            uT_ps[:, a * P:(a + 1) * P],
                            u_sb[:, lead // GROUP % 2, HPC * b + a].rearrange("p g s -> p (g s)"), ident[:])
                    mm.then_inc(s_uT, 1)

            def slot(turn, j):
                base = turn * UNROLL
                if in_range(turn, j, LAG_SCORE):
                    i = j - LAG_SCORE
                    pe.wait_ge(s_xhi, base + i + 1)
                    pe.wait_ge(s_xlo, base + i + 1)
                    if not isinstance(turn, int) or base + i >= 2:
                        pe.wait_ge(s_u1, base + i - 1)
                    z = z_ps[i % 2]
                    nc.tensor.matmul(z[:], pick_c[:], bias_rows[:], start=True, stop=False)
                    three_pass(z, xT_hi, xT_lo, A_hi, A_lo, start=False).then_inc(s_score, 1)
                lead = j - LAG_CHECK
                if lead % GROUP == 0 and in_range(turn, j, LAG_CHECK):
                    pe.wait_ge(s_differs, group_of(turn, lead) + 1)
                    if not isinstance(turn, int) or base + lead > 0:
                        pe.wait_ge(s_p, base + lead)
                    nc.tensor.matmul(uT_ps[0:1, 0:GROUP], ones_col[:], differs[:], start=True,
                                     stop=True).then_inc(s_opens, 1)
                if in_range(turn, j, LAG_X):
                    i = j - LAG_X
                    pe.wait_ge(s_x[i % XR], 16 * (turns_of(turn, j, LAG_X, XR) + 1))
                    if not isinstance(turn, int) or base + i >= 1:
                        pe.wait_ge(s_xhi, base + i)
                        pe.wait_ge(s_xlo, base + i)
                    for c in range(C):
                        mm = nc.tensor.transpose(xT_ps[:, c * P:(c + 1) * P], x_sb[:, i % XR, c * P:(c + 1) * P],
                                                 ident[:])
                    mm.then_inc(s_xT, 1)
                if in_range(turn, j, LAG_YT):
                    i = j - LAG_YT
                    pe.wait_ge(s_y, base + i + 1)
                    if not isinstance(turn, int) or base + i >= 1:
                        pe.wait_ge(s_srow, base + i)
                    if not isinstance(turn, int) or base + i >= 2:
                        pe.wait_ge(s_sc, base + i - 1)
                    for c in range(C):
                        mm = nc.tensor.transpose(ys_ps[:, c * P:(c + 1) * P], y_sb[:, i % YR, c * P:(c + 1) * P],
                                                 ident[:])
                    mm.then_inc(s_yT, 1)
                probabilities(turn, j, 0)
                if in_range(turn, j, LAG_WO):
                    i = j - LAG_WO
                    pe.wait_ge(s_ohi, base + i + 1)
                    pe.wait_ge(s_olo, base + i + 1)
                    if not isinstance(turn, int) or base + i >= 1:
                        pe.wait_ge(s_r1, base + i)
                    three_pass(o_ps, oT_hi, oT_lo, Wo_hi, Wo_lo, start=True).then_inc(s_o, 1)
                if in_range(turn, j, LAG_VALUE):
                    i = j - LAG_VALUE
                    if i % UNROLL == 0:
                        pe.wait_ge(s_p, base + i + UNROLL)
                    if not isinstance(turn, int) or base + i >= 1:
                        pe.wait_ge(s_olo, base + i)
                    nc.tensor.matmul(v_ps[:], V_blk[:, i % H, :],
                                     pT[:, bass.ds(pair_place(turn, i) + i % H * C * P, C * P)],
                                     start=True, stop=True).then_inc(s_v, 1)
                if in_range(turn, j, LAG_YT):
                    i = j - LAG_YT
                    pe.wait_ge(s_yTc, base + i + 1)
                    for c in range(C):
                        mm = nc.tensor.matmul(ys_ps[:, 0:M], yT[:, c, :], Win_sb[:, c, :], start=(c == 0),
                                              stop=(c == C - 1))
                    mm.then_inc(s_s, 1)
                if in_range(turn, j, LAG_S):
                    i = j - LAG_S
                    pe.wait_ge(s_srow, base + i + 1)
                    pe.wait_ge(s_yTc, so_far(turn, j, LAG_YT))
                    if not isinstance(turn, int) or base + i >= 1:
                        pe.wait_ge(s_sc, base + i)
                    nc.tensor.transpose(ys_ps[:, P:2 * P], s_rows[:].rearrange("p a m -> p (a m)"),
                                        ident[:]).then_inc(s_sT, 1)
                probabilities(turn, j, 1)
                if in_range(turn, j, LAG_OUT):
                    i = j - LAG_OUT
                    if i % GROUP == 0:
                        pe.wait_ge(s_acc, (group_of(turn, i) + 1) * KH)
                    if not isinstance(turn, int) or base + i >= 1:
                        pe.wait_ge(s_r2, base + i)
                    q = i % GROUP
                    nc.tensor.matmul(f_ps[:], acc[:, (i // GROUP) % 2, q * P:(q + 1) * P], WoutD[:],
                                     start=True, stop=True).then_inc(s_f, 1)

            slots(pe, slot)

        @block.scalar
        def _(act):
            for n, (name, c) in enumerate(STEPS):
                ps = banks[n % 8]
                act.wait_ge(s_smm, n + 1)
                if name == "kpT":
                    for a in range(HPC):
                        cp = nc.scalar.copy(kpT4[:, c, a * S:(a + 1) * S], ps[:, 0:S])
                    cp.then_inc(s_sev, 1)
                elif name == "keysT":
                    nc.scalar.activation(keysT4[:, c, :], ps[:, 0:P], ACT.Identity,
                                         bias=bk_c[:, c:c + 1]).then_inc(s_sev, 1)
                elif name == "V":
                    act.wait_ge(s_const, CONSTS)
                    for a in range(HPC):
                        rows = slice(a * S, (a + 1) * S)
                        cp = nc.scalar.copy(V_blk[rows, :, rows], ps[rows, :].rearrange("p (h d) -> p h d", h=H))
                    cp.then_inc(s_sev, 1)
                elif name == "WqT":
                    nc.scalar.copy(WqT[:, c, :], ps[:]).then_inc(s_sev, 1)
                elif name == "c":
                    nc.scalar.mul(c_full, ps[0:1, :], SCALE).then_inc(s_sev, 1)
                else:
                    nc.scalar.mul(A_f[:, c, :], ps[:], SCALE).then_inc(s_sev, 1)

            def probabilities(turn, j, half):
                for lead, b in batches(turn, j, half):
                    base = turn * UNROLL
                    jc, h0 = (lead // GROUP) % C, HPC * b
                    act.wait_ge(s_uT, base + lead + b + 1)
                    if not isinstance(turn, int) or base + lead >= 2 * UNROLL:
                        act.wait_ge(s_v, base + (lead - lead % UNROLL) - 2 * UNROLL + h0 + HPC)
                    place = pT[:, bass.ds(pair_place(turn, lead) + h0 * C * P, HPC * C * P)]
                    nc.scalar.activation(place.rearrange("p (a c n) -> p a c n", a=HPC, c=C)[:, :, jc, :],
                                         uT_ps[:].rearrange("p (a n) -> p a n", a=HPC),
                                         ACT.Relu).then_inc(s_p, 1)

            def square(turn, j, lag, s_mean, s_before, n_before, shift_sq, s_ve, var, s_var):
                i = j - lag
                t0 = turn * UNROLL + i + 1
                act.wait_ge(s_mean, 2 * t0)
                if not isinstance(t0, int) or t0 >= 3:
                    act.wait_ge(s_ve, t0 - 2)
                if not isinstance(n_before, int) or n_before > 0:
                    act.wait_ge(s_before, n_before)
                nc.scalar.activation(unread[:], y_sb[:, i % YR, :], ACT.Square,
                                     bias=shift_sq[:, i % 2:i % 2 + 1], scale=1.0 / D ** 0.5,
                                     accum_out=var[:, i % 2:i % 2 + 1]).then_inc(s_var, 1)

            def make_hinge(turn, j, half):
                i = j - LAG_HINGE
                lead = i - i % GROUP
                if not in_range(turn, 0, -lead):
                    return
                base, g, k = turn * UNROLL, group_of(turn, lead), 2 * (i % GROUP) + half
                if k == 0:
                    act.wait_ge(s_sc, base + lead + GROUP)
                if not isinstance(turn, int) or base + lead > 0 or k >= HR:
                    act.wait_ge(s_acc, g * KH + k - HR + 1)
                nc.scalar.activation(hinge[:, k % HR, :], s_sb[:, (lead // GROUP) % 2, :], ACT.Relu,
                                     bias=b1c[:, k:k + 1], scale=w1c[:, k:k + 1]).then_inc(s_hinge, 1)

            def slot(turn, j):
                base = turn * UNROLL
                if in_range(turn, j, LAG_WO):
                    i = j - LAG_WO
                    act.wait_ge(s_v, base + i + 1)
                    if not isinstance(turn, int) or base + i >= 1:
                        act.wait_ge(s_o, base + i)
                    nc.scalar.copy(oT_hi[:].rearrange("p c n -> p (c n)"), v_ps[:]).then_inc(s_ohi, 1)
                if in_range(turn, j, LAG_S):
                    i = j - LAG_S
                    act.wait_ge(s_s, base + i + 1)
                    if not isinstance(turn, int) or base + i >= 1:
                        act.wait_ge(s_sT, base + i)
                    nc.scalar.copy(s_rows[:], ys_ps[:, 0:M].unsqueeze(1).broadcast_to([P, 2, M])).then_inc(s_srow, 1)
                if in_range(turn, j, LAG_SC):
                    i = j - LAG_SC
                    par, q = (i // GROUP) % 2, i % GROUP
                    act.wait_ge(s_sT, base + i + 1)
                    if not isinstance(turn, int) or base + i >= 2 * GROUP:
                        act.wait_ge(s_hinge, (group_of(turn, i) - 1) * KH)
                    nc.scalar.activation(s_sb[:, par, q * P:(q + 1) * P], ys_ps[:, P:2 * P], ACT.Identity,
                                         bias=bin2[:]).then_inc(s_sc, 1)
                if in_range(turn, j, LAG_FINAL):
                    i = j - LAG_FINAL
                    act.wait_ge(s_shift2, base + i + 1)
                    if not isinstance(turn, int) or base + i >= OR:
                        act.wait_ge(s_store[i % OR], 32 * turns_of(turn, j, LAG_FINAL, OR))
                    nc.scalar.activation(o_sb[:, i % OR, :], y_sb[:, i % YR, :], ACT.Identity,
                                         bias=shift2[:, i % 2:i % 2 + 1], scale=rstd2[:, i % 2:i % 2 + 1]
                                         ).then_inc(s_final, 1)
                if in_range(turn, j, LAG_Y):
                    i = j - LAG_Y
                    act.wait_ge(s_shift1, base + i + 1)
                    nc.scalar.activation(y_sb[:, i % YR, :], y_sb[:, i % YR, :], ACT.Identity,
                                         bias=shift1[:, i % 2:i % 2 + 1], scale=rstd1[:, i % 2:i % 2 + 1]
                                         ).then_inc(s_y, 1)
                if in_range(turn, j, LAG_COUNT):
                    i = j - LAG_COUNT
                    act.wait_ge(s_u, base + i + 1)
                    if (not isinstance(turn, int) or base + i >= UR) and i % GROUP == 0:
                        act.wait_ge(s_differs, group_of(turn, i) - 1)
                    if not isinstance(turn, int) or base + i >= 1:
                        act.wait_ge(s_count2, base + i)
                    for s_var, lag in ((s_var1, LAG_NORM1), (s_var2, LAG_NORM2)):
                        squares = so_far(turn, j - 1, lag)
                        if not isinstance(turn, int) or squares > 0:
                            act.wait_ge(s_var, squares)
                    nc.scalar.activation(by_head(unread[:]), u_of(i), ACT.Sign,
                                         accum_out=count2[:, i % UR:i % UR + 1]).then_inc(s_count2, 1)
                if in_range(turn, j, LAG_X):
                    i = j - LAG_X
                    act.wait_ge(s_xT, base + i + 1)
                    if not isinstance(turn, int) or base + i >= 1:
                        act.wait_ge(s_score, base + i)
                    nc.scalar.copy(xT_hi[:].rearrange("p c n -> p (c n)"), xT_ps[:]).then_inc(s_xhi, 1)
                if in_range(turn, j, LAG_YT):
                    i = j - LAG_YT
                    act.wait_ge(s_yT, base + i + 1)
                    if not isinstance(turn, int) or base + i >= 1:
                        act.wait_ge(s_s, base + i)
                    nc.scalar.copy(yT[:].rearrange("p c n -> p (c n)"), ys_ps[:]).then_inc(s_yTc, 1)
                probabilities(turn, j, 0)
                if in_range(turn, j, LAG_SIDE):
                    i = j - LAG_SIDE
                    act.wait_ge(s_u1, base + i + 1)
                    if not isinstance(turn, int) or base + i >= 1:
                        act.wait_ge(s_sums, base + i)
                        act.wait_ge(s_sumc, base + i)
                    if (not isinstance(turn, int) or base + i >= UR) and i % GROUP == 0:
                        act.wait_ge(s_differs, group_of(turn, i) - 1)
                    nc.scalar.activation(side[:], u_raw[:, i % 2, :], ACT.Sign,
                                         accum_out=count1[:, i % UR:i % UR + 1]).then_inc(s_side, 1)
                    nc.scalar.activation(above[:], u_raw[:, i % 2, :], ACT.Relu).then_inc(s_above, 1)
                if in_range(turn, j, LAG_NORM1):
                    square(turn, j, LAG_NORM1, s_mean1, s_count2, so_far(turn, j, LAG_COUNT), shift_sq1, s_ve1,
                           var1, s_var1)
                make_hinge(turn, j, 0)
                if in_range(turn, j, LAG_NORM2):
                    square(turn, j, LAG_NORM2, s_mean2, s_var1, so_far(turn, j, LAG_NORM1), shift_sq2, s_ve2,
                           var2, s_var2)
                make_hinge(turn, j, 1)
                probabilities(turn, j, 1)

            slots(act, slot)

        @block.vector
        def _(dve):
            dve.wait_ge(s_const, CONSTS)
            dve.wait_ge(s_sev, done("keysT"))
            for c in range(C):
                for a in range(HPC):
                    rows = slice(a * S, (a + 1) * S)
                    cp = nc.vector.tensor_copy(K_blk[rows, c, rows], keysT4[rows, c, 0:S])
                cp.then_inc(s_blk, 1)
            dve.wait_ge(s_sev, done("c"))
            nc.vector.tensor_copy(bias_rows[0:1, :], c_full).then_inc(s_c, 1)
            dve.wait_ge(s_c, 1)
            nc.vector.tensor_tensor(bias_rows[E:E + 1, :], c_full, bias_rows[0:1, :].bitcast(F32),
                                    ALU.subtract).then_inc(s_c, 1)
            for n, (full, hi, lo, ready) in enumerate(((Wo_sb, Wo_hi, Wo_lo, 0), (A_f, A_hi, A_lo, done("A")))):
                if ready:
                    dve.wait_ge(s_sev, ready)
                nc.vector.tensor_copy(hi[:], full).then_inc(s_ready, 1)
                dve.wait_ge(s_ready, 2 * n + 1)
                nc.vector.tensor_tensor(lo[:], full, hi[:].bitcast(F32), ALU.subtract).then_inc(s_ready, 1)

            def spread(row):
                return row.unsqueeze(2).broadcast_to([P, H, S])

            def sort_tile(par, q):
                with dve.Fori(0, H // HPC) as quarter:
                    block = u_flat[:, bass.ds(quarter * (HPC * GROUP * S) + par * (H * GROUP * S), HPC * GROUP * S)]
                    scores = block.rearrange("p (h g s) -> p h g s", h=HPC, g=GROUP)[:, :, q, :]
                    nc.vector.tensor_copy(rest, scores)
                    dve.drain()
                    for r in range(0, S, TOP):
                        for a in range(HPC):
                            nc.vector.max(ranked[:, a, r:r + TOP], rest[:, a, :])
                        dve.drain()
                        for a in range(HPC if r + TOP < S else 0):
                            nc.vector.match_replace(rest[:, a, :], ranked[:, a, r:r + TOP], rest[:, a, :], LOWEST)
                        dve.drain()
                    for a in range(HPC):
                        nc.vector.tensor_tensor_scan(rest[:, a, :], ones_s[:], ranked[:, a, :], 0.0, ALU.mult,
                                                     ALU.add)
                    dve.drain()
                    nc.vector.scalar_tensor_tensor(rest, rest, -1.0, rank_inv[:].unsqueeze(1).broadcast_to(
                        [P, HPC, S]), ALU.add, ALU.mult)
                    dve.drain()
                    nc.vector.tensor_reduce(tau_some[:], rest, AX.X, ALU.max)
                    dve.drain()
                    nc.vector.scalar_tensor_tensor(scores, tau_some[:].unsqueeze(2).broadcast_to([P, HPC, S]), -1.0,
                                                   scores, ALU.mult, ALU.add)
                    dve.drain()

            def residual(t1, ps, s_prod, other, s_other, n_other, rows, total, s_mean, s_rows):
                dve.wait_ge(s_prod, t1)
                dve.wait_ge(s_other, n_other)
                if not isinstance(t1, int) or t1 >= 3:
                    dve.wait_ge(s_mean, 2 * t1 - 4)
                nc.vector.scalar_tensor_tensor(rows, ps[:], 0.0, other, ALU.add, ALU.add,
                                               accum_out=total).then_inc(s_rows, 1)

            def lower_half(row):
                return by_head(row[:])[:, :, 0:S // 2]

            def slot(turn, j):
                base = turn * UNROLL
                lead = j - LAG_CHECK
                checks = lead % GROUP == 0 and in_range(turn, j, LAG_CHECK)
                if in_range(turn, j, LAG_WO):
                    i = j - LAG_WO
                    dve.wait_ge(s_ohi, base + i + 1)
                    nc.vector.tensor_tensor(
                        oT_lo[:].rearrange("p c n -> p (c n)"), v_ps[:],
                        oT_hi[:].bitcast(F32).rearrange("p c n -> p (c n)"), ALU.subtract
                    ).then_inc(s_olo, 1)
                if checks:
                    g = group_of(turn, lead)
                    dve.wait_ge(s_count2, base + lead + GROUP)
                    if not isinstance(turn, int) or base + lead > 0:
                        dve.wait_ge(s_opens, g)
                    places = slice(lead % UR, lead % UR + GROUP)
                    nc.vector.tensor_tensor(differs[:], count1[:, places], count2[:, places],
                                            ALU.not_equal).then_inc(s_differs, 1)
                if in_range(turn, j, LAG_STEP):
                    t1 = base + (j - LAG_STEP) + 1
                    dve.wait_ge(s_foldc, t1)
                    nc.vector.tensor_reduce(sum_side[:], lower_half(side), AX.X, ALU.add).then_inc(s_sumc, 1)
                    dve.wait_ge(s_folds, t1)
                    nc.vector.tensor_reduce(sum_above[:], lower_half(above), AX.X, ALU.add).then_inc(s_sums, 1)
                    dve.wait_ge(s_sumc, t1)
                    nc.vector.tensor_scalar(twice[:], sum_side[:], float(S), 2.0, ALU.add, ALU.max).then_inc(s_twice, 1)
                if in_range(turn, j, LAG_NORM1):
                    i = j - LAG_NORM1
                    if not isinstance(turn, int) or base + i >= YR:
                        dve.wait_ge(s_final, base + i - YR + 1)
                    residual(base + i + 1, o_ps, s_o, xr_sb[:, i % RR, :], s_xb, base + i + 1, y_sb[:, i % YR, :],
                             sum1[:, i % 2:i % 2 + 1], s_mean1, s_r1)
                if in_range(turn, j, LAG_STEP):
                    t1 = base + (j - LAG_STEP) + 1
                    dve.wait_ge(s_twice, t1)
                    nc.vector.reciprocal(twice_inv[:], twice[:]).then_inc(s_inv, 1)
                if in_range(turn, j, LAG_NORM2):
                    i = j - LAG_NORM2
                    residual(base + i + 1, f_ps, s_f, y_sb[:, i % YR, :], s_yb, base + i + 1,
                             y_sb[:, i % YR, :], sum2[:, i % 2:i % 2 + 1], s_mean2, s_r2)
                if in_range(turn, j, LAG_STEP):
                    t1 = base + (j - LAG_STEP) + 1
                    dve.wait_ge(s_sums, t1)
                    dve.wait_ge(s_inv, t1)
                    nc.vector.scalar_tensor_tensor(step[:], sum_above[:], -1.0, twice_inv[:], ALU.add,
                                                   ALU.mult).then_inc(s_step, 1)
                if in_range(turn, j, LAG_STEP):
                    i = j - LAG_STEP
                    dve.wait_ge(s_step, base + i + 1)
                    if not isinstance(base, int) or base + i >= UR:
                        dve.wait_ge(s_uT, base + (i - i % GROUP) - UR + GROUP)
                    nc.vector.scalar_tensor_tensor(u_of(i), spread(step[:]), -2.0, by_head(u_raw[:, i % 2, :]),
                                                   ALU.mult, ALU.add).then_inc(s_u, 1)
                if in_range(turn, j, LAG_SCORE) and not isinstance(turn, int):
                    dve.wait_ge(s_score, base + (j - LAG_SCORE) + 1)
                if in_range(turn, j, LAG_X):
                    i = j - LAG_X
                    dve.wait_ge(s_xhi, base + i + 1)
                    nc.vector.tensor_tensor(
                        xT_lo[:].rearrange("p c n -> p (c n)"), xT_ps[:],
                        xT_hi[:].bitcast(F32).rearrange("p c n -> p (c n)"), ALU.subtract
                    ).then_inc(s_xlo, 1)
                if in_range(turn, j, LAG_SCORE):
                    i = j - LAG_SCORE
                    if isinstance(turn, int):
                        dve.wait_ge(s_score, base + i + 1)
                    for h in range(H):
                        mx = nc.vector.max(top8[:, h, :], z_ps[i % 2][:, h * S:(h + 1) * S])
                    mx.then_inc(s_top, 1)
                if in_range(turn, j, LAG_SCORE):
                    i = j - LAG_SCORE
                    dve.wait_ge(s_top, base + i + 1)
                    nc.vector.tensor_tensor_scan(cum[:].rearrange("p h k -> p (h k)"),
                                                 go_on[:].rearrange("p h k -> p (h k)"),
                                                 top8[:].rearrange("p h k -> p (h k)"), 0.0,
                                                 ALU.mult, ALU.add).then_inc(s_cum, 1)
                hinge_step(turn, j, 0)
                if in_range(turn, j, LAG_SCORE):
                    i = j - LAG_SCORE
                    dve.wait_ge(s_cum, base + i + 1)
                    nc.vector.scalar_tensor_tensor(cum[:], cum[:], -1.0, rank_inv[:, 0:TOP].unsqueeze(1).broadcast_to([P, H, TOP]), ALU.add,
                                                   ALU.mult).then_inc(s_cand, 1)
                hinge_step(turn, j, 1)
                if in_range(turn, j, LAG_SCORE):
                    i = j - LAG_SCORE
                    dve.wait_ge(s_cand, base + i + 1)
                    nc.vector.tensor_reduce(tau[:], cum[:], AX.X, ALU.max).then_inc(s_tau, 1)
                    dve.wait_ge(s_tau, base + i + 1)
                    if not isinstance(base, int) or base + i >= 2:
                        dve.wait_ge(s_u, base + i - 1)
                    nc.vector.tensor_tensor(by_head(u_raw[:, i % 2, :]), by_head(z_ps[i % 2][:]),
                                            spread(tau[:]), ALU.subtract).then_inc(s_u1, 1)
                if checks:
                    g = group_of(turn, lead)
                    dve.wait_ge(s_opens, g + 1)
                    nc.vector.tensor_copy(open_tiles[:], uT_ps[0:1, 0:GROUP]).then_inc(s_openr, 1)
                    nc.vector.tensor_reduce(open_any[:], uT_ps[0:1, 0:GROUP], AX.X, ALU.max).then_inc(s_openr, 1)
                    dve.drain()
                    with dve.If(dve.value_load(open_any[:], min_val=0, max_val=P) > 0):
                        for q in range(GROUP):
                            with dve.If(dve.value_load(open_tiles[:, q:q + 1], min_val=0, max_val=P) > 0):
                                sort_tile(lead // GROUP % 2, q)
                    dve.nop().then_inc(s_checked, 1)

            def hinge_step(turn, j, half):
                base = turn * UNROLL
                i = j - LAG_HINGE
                first = i - i % GROUP
                if not in_range(turn, 0, -first):
                    return
                g, par, k = group_of(turn, first), (first // GROUP) % 2, 2 * (i % GROUP) + half
                dve.wait_ge(s_hinge, g * KH + k + 1)
                if k == 0:
                    if not isinstance(base, int) or base + first >= 2 * GROUP:
                        dve.wait_ge(s_f, base + first - GROUP)
                    nc.vector.tensor_scalar(acc[:, par, :], hinge[:, k % HR, :], w2c[:, k:k + 1], b2c[:],
                                            ALU.mult, ALU.add).then_inc(s_acc, 1)
                else:
                    dve.wait_ge(s_acc, g * KH + k)
                    nc.vector.scalar_tensor_tensor(acc[:, par, :], hinge[:, k % HR, :], w2c[:, k:k + 1],
                                                   acc[:, par, :], ALU.mult, ALU.add).then_inc(s_acc, 1)

            slots(dve, slot)


_INS = ['query', 'key_param', 'Wq', 'bq', 'Wk', 'bk', 'Wv', 'bv', 'Wo', 'bo']
_FFN = ['Win', 'bin_', 'W1', 'b1', 'W2', 'b2', 'Wout', 'bout']
_NAMES = ['L0_attn_' + n for n in _INS] + ['L0_ffn_' + n for n in _FFN]
_OUTS = [((16, 1024, 512), 'float32')]


def kernel(**inputs):
    import numpy as _np
    import concourse.bacc as _bacc
    from concourse import mybir as _mybir
    from concourse.bass_utils import run_bass_kernel_spmd as _run

    nc = _bacc.Bacc("TRN2", target_bir_lowering=False, num_devices=1)
    arrays, args = {}, []
    for name in _NAMES:
        a = _np.ascontiguousarray(inputs[name])
        arrays[f"in_{name}_dram"] = a
        args.append(nc.dram_tensor(f"in_{name}_dram", a.shape, _mybir.dt.from_np(a.dtype), kind="ExternalInput").ap())
    for i, (shape, dtype) in enumerate(_OUTS):
        dt = _mybir.dt.from_np(_np.dtype(dtype))
        args.append(nc.dram_tensor(f"out_{i}_dram", shape, dt, kind="ExternalOutput").ap())
    build_kernel(nc, *args)
    r = _run(nc, [arrays], core_ids=[0])
    got = tuple(r.results[0][f"out_{i}_dram"] for i in range(len(_OUTS)))
    return got[0]
```

```python
from contextlib import ExitStack

import concourse.bass as bass
from concourse import mybir

F32 = mybir.dt.float32
F32R = mybir.dt.float32r
BF16 = mybir.dt.bfloat16
I32 = mybir.dt.int32
ALU = mybir.AluOpType
ACT = mybir.ActivationFunctionType
AX = mybir.AxisListType

P = 128
GROUP = 4
UNROLL = 16
LOWEST = -3.0e38
EPS = 1e-5

LAG_X = 0
LAG_SCORE = 1
LAG_SIDE = 2
LAG_STEP = 3
LAG_COUNT = 4
LAG_CHECK = 8
LAG_PROB = 9
LAG_VALUE = 24
LAG_XB = 25
LAG_WO = 25
LAG_NORM1 = 26
LAG_Y = 27
LAG_YT = 28
LAG_S = 29
LAG_HINGE = 32
LAG_SPLIT = 36
LAG_OUT = 36
LAG_NORM2 = 37
LAG_FINAL = 38
FILL = 3


def build_kernel(nc, query, key_param, Wq, bq, Wk, bk, Wv, bv, Wo, bo,
                 Win, bin_, W1, b1, W2, b2, Wout, bout, out):
    B, L, D = query.shape
    S = key_param.shape[1]
    M, INNER = W1.shape
    HD = Wq.shape[1]
    E = 32
    H = HD // E
    C = D // P
    TILES = B * L // P
    KH = M * INNER // P
    HPC = P // S
    SCALE = 1.0 / float(E) ** 0.5
    TOP = 8
    assert D == HD == H * S == 512 and E == S == 32 and M * 2 == P and TILES % UNROLL == 0

    HALF = L // H
    assert 2 * HALF == P and L // H * H == L and TILES == B // 2 * UNROLL and H == UNROLL
    x_tiles = query.rearrange("(q b) (r j) d -> q j (b r) d", b=2, j=H)
    x_rows = query.rearrange("(q b) (h r) d -> q h b r d", b=2, h=H)
    out_rows = out.rearrange("(q b) (h r) d -> q h b r d", b=2, h=H)

    with ExitStack() as ctx:
        def sb(name, shape, dt=F32):
            return ctx.enter_context(nc.sbuf_tensor(name, shape, dt))

        def sem(name):
            return ctx.enter_context(nc.semaphore(name))

        XR, YR, OR, UR, HR = 2, 16, 2, 8, 2
        x_sb = sb("x_sb", [P, XR, D])
        xT_hi = sb("xT_hi", [P, C, P], F32R)
        xT_lo = sb("xT_lo", [P, C, P], F32R)
        top8 = sb("top8", [P, H, TOP])
        cum = sb("cum", [P, H, TOP])
        tau = sb("tau", [P, H])
        u_sb = sb("u_sb", [P, UR // GROUP, H, GROUP, S])
        u_raw = sb("u_raw", [P, 2, D])
        u_flat = u_sb[:].rearrange("p a h g s -> p (a h g s)")
        above = sb("above", [P, D])
        side = sb("side", [P, D], BF16)
        unread = sb("unread", [P, D], BF16)
        count1 = sb("count1", [P, UR])
        count2 = sb("count2", [P, UR])
        sum_above = sb("sum_above", [P, H])
        sum_side = sb("sum_side", [P, H])
        twice = sb("twice", [P, H])
        twice_inv = sb("twice_inv", [P, H])
        step = sb("step", [P, H])
        differs = sb("differs", [P, GROUP])
        open_tiles = sb("open_tiles", [1, GROUP], I32)
        open_any = sb("open_any", [1, 1], I32)
        ones_col = sb("ones_col", [P, 1])
        pT = sb("pT", [P, 2 * H * C * P])
        oT_hi = sb("oT_hi", [P, C, P], F32R)
        oT_lo = sb("oT_lo", [P, C, P], F32R)
        sum1 = sb("sum1", [P, 2])
        minus_mean1 = sb("minus_mean1", [P, 2])
        shift_sq1 = sb("shift_sq1", [P, 2])
        var1 = sb("var1", [P, 2])
        ve1 = sb("ve1", [P, 1])
        rstd1 = sb("rstd1", [P, 2])
        shift1 = sb("shift1", [P, 2])
        y_sb = sb("y_sb", [P, YR, D])
        yT = sb("yT", [P, C, P])
        s_sb = sb("s_sb", [P, 2, GROUP * P])
        hinge = sb("hinge", [P, HR, GROUP * P])
        acc = sb("acc", [P, GROUP * P])
        acc_lo = sb("acc_lo", [P, GROUP * P], F32R)
        acc_hi = sb("acc_hi", [P, GROUP * P], F32R)
        sum2 = sb("sum2", [P, 2])
        minus_mean2 = sb("minus_mean2", [P, 2])
        shift_sq2 = sb("shift_sq2", [P, 2])
        var2 = sb("var2", [P, 2])
        ve2 = sb("ve2", [P, 1])
        rstd2 = sb("rstd2", [P, 2])
        shift2 = sb("shift2", [P, 2])
        o_sb = sb("o_sb", [P, OR, D])
        A_hi = sb("A_hi", [P, C, D], F32R)
        A_lo = sb("A_lo", [P, C, D], F32R)
        Wo_hi = sb("Wo_hi", [P, C, D], F32R)
        Wo_lo = sb("Wo_lo", [P, C, D], F32R)
        V_blk = sb("V_blk", [P, H, P])
        bias_rows = sb("bias_rows", [P, D], F32R)
        pick_c = sb("pick_c", [P, P], F32R)
        bo_bc = sb("bo_bc", [P, D])
        Win_sb = sb("Win_sb", [P, C, M])
        Wout_hi = sb("Wout_hi", [P, D], F32R)
        Wout_lo = sb("Wout_lo", [P, D], F32R)
        bout_bc = sb("bout_bc", [P, D])
        bin_sb = sb("bin_sb", [M, 1])
        w1c = sb("w1c", [P, KH])
        b1c = sb("b1c", [P, KH])
        w2c = sb("w2c", [P, KH])
        b2c = sb("b2c", [P, 1])
        ident = sb("ident", [P, P])
        go_on = sb("go_on", [P, H, TOP])
        rank_inv = sb("rank_inv", [P, S])
        minus_half = sb("minus_half", [P, 1])
        eps = sb("eps", [P, 1])
        per_row = sb("per_row", [P, 1])
        per_row_sq = sb("per_row_sq", [P, 1])
        rest = cum[:].rearrange("p h k -> p (h k)").rearrange("p (a s) -> p a s", s=S)
        ranked = top8[:].rearrange("p h k -> p (h k)").rearrange("p (a s) -> p a s", s=S)
        ones_s = sb("ones_s", [P, S])
        tau_some = sb("tau_some", [P, HPC])
        Wk_sb, Wv_sb, Wq_sb, Wo_sb = (y_sb[:, n * C:(n + 1) * C, :] for n in range(4))
        A_f, WqT = (u_flat[:, n * C * D:(n + 1) * C * D].rearrange("p (c n) -> p c n", c=C) for n in range(2))
        kp_sb, c_full, bv_row = (
            hinge[0:S, 0, :], hinge[0:1, 1, :], s_sb[0:1, 1, :])
        Wout_sb = s_sb[:, 0, :]
        K_blk = acc[:].rearrange("p (c n) -> p c n", c=C)
        bk_c = sb("bk_c", [P, C])
        bq_c = sb("bq_c", [P, C])
        ones_row = above[0:1, 0:P]
        kpT4, keysT4 = (r.rearrange("p (c n) -> p c n", c=C) for r in (o_sb[:, 0, :], o_sb[:, 1, :]))

        banks = [ctx.enter_context(nc.psum_tensor(f"bank{i}", [P, 512], F32)) for i in range(8)]
        xT_ps, z_ps, uT_ps, v_ps, o_ps, ys_ps, f_ps = (
            banks[0], [banks[1], banks[2]], banks[3], banks[4], banks[5], banks[6], banks[7])

        s_x = [sem(f"s_x{i}") for i in range(XR)]
        s_store = [sem(f"s_store{i}") for i in range(OR)]
        s_xT, s_xhi, s_xlo = sem("s_xT"), sem("s_xhi"), sem("s_xlo")
        s_score, s_top, s_cum, s_cand, s_tau = sem("s_score"), sem("s_top"), sem("s_cum"), sem("s_cand"), sem("s_tau")
        s_u1, s_above, s_side, s_sums, s_sumc, s_twice, s_inv, s_step = (
            sem("s_u1"), sem("s_above"), sem("s_side"), sem("s_sums"), sem("s_sumc"), sem("s_twice"),
            sem("s_inv"), sem("s_step"))
        s_step2 = sem("s_step2")
        s_count2 = sem("s_count2")
        s_differs, s_opens, s_checked = (
            sem("s_differs"), sem("s_opens"), sem("s_checked"))
        s_u, s_uT, s_p, s_v, s_ohi, s_olo, s_o = (
            sem("s_u"), sem("s_uT"), sem("s_p"), sem("s_v"), sem("s_ohi"), sem("s_olo"), sem("s_o"))
        s_xr = [sem(f"s_xr{i}") for i in range(YR)]
        s_r1, s_mean1, s_var1, s_ve1, s_rstd1, s_shift1 = (
            sem("s_r1"), sem("s_mean1"), sem("s_var1"), sem("s_ve1"), sem("s_rstd1"), sem("s_shift1"))
        s_xb = sem("s_xb")
        s_y, s_yb, s_yT, s_yTc, s_s = sem("s_y"), sem("s_yb"), sem("s_yT"), sem("s_yTc"), sem("s_s")
        s_sc = sem("s_sc")
        s_hinge, s_acc = sem("s_hinge"), sem("s_acc")
        s_acchi, s_acclo = sem("s_acchi"), sem("s_acclo")
        s_f, s_r2, s_mean2, s_var2 = sem("s_f"), sem("s_r2"), sem("s_mean2"), sem("s_var2")
        s_foldc, s_folds = sem("s_foldc"), sem("s_folds")
        s_ve2, s_rstd2, s_shift2, s_final = sem("s_ve2"), sem("s_rstd2"), sem("s_shift2"), sem("s_final")
        s_const, s_wload, s_smm, s_sev, s_ready = (
            sem("s_const"), sem("s_wload"), sem("s_smm"), sem("s_sev"), sem("s_ready"))
        s_wkeys, s_wq = sem("s_wkeys"), sem("s_wq")
        s_zero, s_blk, s_c = sem("s_zero"), sem("s_blk"), sem("s_c")

        block = ctx.enter_context(nc.Block())
        SLOTS = TILES + FILL * UNROLL

        def slots(eng, slot):
            for turn in range(FILL):
                for j in range(UNROLL):
                    slot(turn, j)
            with eng.Fori(FILL, TILES // UNROLL) as turn:
                for j in range(UNROLL):
                    slot(turn, j)
            for turn in range(TILES // UNROLL, SLOTS // UNROLL):
                for j in range(UNROLL):
                    slot(turn, j)

        def in_range(turn, j, lag):
            return not isinstance(turn, int) or 0 <= turn * UNROLL + j - lag < TILES

        def pool_steps(turn, j):
            return isinstance(turn, int) and turn * UNROLL + j < LAG_VALUE

        def vector_finishes(turn):
            return isinstance(turn, int) and turn >= TILES // UNROLL

        def so_far(turn, j, lag):
            n = turn * UNROLL + j - lag + 1
            return min(max(n, 0), TILES) if isinstance(n, int) else n

        def pair_place(turn, i):
            return (turn + i // UNROLL) % 2 * (H * C * P)

        def turns_of(turn, j, lag, ring):
            return turn * (UNROLL // ring) + (j - lag) // ring

        def batches(turn, j, half):
            lead = j - LAG_PROB
            if lead % GROUP < 2 and in_range(turn, j, LAG_PROB):
                yield lead - lead % GROUP, 2 * (lead % GROUP) + half

        def u_of(i):
            return u_sb[:, i // GROUP % 2, :, i % GROUP, :]

        def spread(row):
            return row.unsqueeze(2).broadcast_to([P, H, S])

        def by_head(row):
            return row.rearrange("p (h s) -> p h s", h=H)

        def group_of(turn, i):
            return turn * (UNROLL // GROUP) + i // GROUP

        KEY_LOADS, Q_LOADS, WLOADS = 3, 2, 16
        FILLS = 13 + S
        CONSTS = FILLS + 4

        @block.sync
        def _(sp):
            loads = [
                (kp_sb, key_param[0]),
                (Wk_sb, Wk.rearrange("(c p) n -> p c n", p=P)),
                (bk_c[:], bk.rearrange("(c p) -> p c", p=P)),
                (Wq_sb, Wq.rearrange("(c p) n -> p c n", p=P)),
                (bq_c[:], bq.rearrange("(c p) -> p c", p=P)),
                (Wv_sb, Wv.rearrange("(c p) n -> p c n", p=P)),
                (bv_row, bv.rearrange("(a d) -> a d", a=1)),
                (Wo_sb, Wo.rearrange("(c p) n -> p c n", p=P)),
                (bo_bc[:], bo.rearrange("(a d) -> a d", a=1).broadcast_to([P, D])),
                (Win_sb[:], Win.rearrange("(c p) m -> p c m", p=P)),
                (bout_bc[:], bout.rearrange("(a d) -> a d", a=1).broadcast_to([P, D])),
                (bin_sb[:], bin_.rearrange("(m a) -> m a", a=1)),
                (b2c[0:M, :], b2.rearrange("(m a) -> m a", a=1)),
            ]
            for j in range(2):
                half = slice(j * M, (j + 1) * M)
                loads += [
                    (Wout_sb[half, :], Wout),
                    (w1c[half, :], W1[:, j * KH:(j + 1) * KH]),
                    (b1c[half, :], b1[:, j * KH:(j + 1) * KH]),
                    (w2c[half, :], W2[:, j * KH:(j + 1) * KH]),
                ]
            sp.wait_ge(s_zero, 1)
            for n, (dst, src) in enumerate(loads):
                s_load = s_wkeys if n < KEY_LOADS else s_wq if n < KEY_LOADS + Q_LOADS else s_wload
                sp.dma_start(dst, src, allow_slow_non_contiguous=True).then_inc(s_load, 16)
            assert len(loads) == KEY_LOADS + Q_LOADS + WLOADS

            LAG_STORE = LAG_FINAL + 2

            def slot(turn, j):
                base = turn * UNROLL
                if in_range(turn, j, 0):
                    tile = x_tiles[turn, j]
                    if not isinstance(turn, int) or base + j >= XR:
                        sp.wait_ge(s_xT, base + j - XR + 1)
                    sp.dma_start(x_sb[:, j % XR, :], tile).then_inc(s_x[j % XR], 16)
                if in_range(turn, j, LAG_XB):
                    i = j - LAG_XB
                    halves = [x_rows[turn + i // H, i % H, half] for half in range(2)]
                    if not isinstance(turn, int) or base + i >= YR:
                        sp.wait_ge(s_final, base + i - YR + 1)
                    for half in range(2):
                        sp.dma_start(y_sb[half * HALF:(half + 1) * HALF, i % YR, :], halves[half]).then_inc(
                            s_xr[i % YR], 16)
                if in_range(turn, j, LAG_STORE):
                    i = j - LAG_STORE
                    halves = [out_rows[turn + i // H, i % H, half] for half in range(2)]
                    sp.wait_ge(s_final, base + i + 1)
                    for half in (1, 0):
                        sp.dma_start(halves[half], o_sb[half * HALF:(half + 1) * HALF, i % OR, :]).then_inc(
                                         s_store[i % OR], 16)

            slots(sp, slot)
            for r in range(OR):
                sp.wait_ge(s_store[r], 32 * (TILES // OR))

        @block.gpsimd
        def _(pool):
            nc.gpsimd.memset(b2c[:], 0.0).then_inc(s_zero, 1)
            nc.gpsimd.memset(ident[:], 0.0).then_inc(s_const, 1)
            nc.gpsimd.memset(go_on[:], 1.0).then_inc(s_const, 1)
            nc.gpsimd.memset(ones_s[:], 1.0).then_inc(s_const, 1)
            nc.gpsimd.memset(K_blk, 0.0).then_inc(s_const, 1)
            nc.gpsimd.memset(V_blk[:], 0.0).then_inc(s_const, 1)
            nc.gpsimd.memset(bias_rows[:].bitcast(F32), 0.0).then_inc(s_const, 1)
            nc.gpsimd.memset(pick_c[:].bitcast(F32), 0.0).then_inc(s_const, 1)
            nc.gpsimd.memset(ones_row, 1.0).then_inc(s_const, 1)
            nc.gpsimd.memset(minus_half[:], -0.5).then_inc(s_const, 1)
            nc.gpsimd.memset(eps[:], EPS).then_inc(s_const, 1)
            nc.gpsimd.memset(per_row[:], -1.0 / D).then_inc(s_const, 1)
            nc.gpsimd.memset(per_row_sq[:], -1.0 / D ** 1.5).then_inc(s_const, 1)
            for k in range(S):
                nc.gpsimd.memset(rank_inv[:, k:k + 1], 1.0 / (k + 1)).then_inc(s_const, 1)
            nc.gpsimd.memset(ones_col[:], 1.0).then_inc(s_const, 1)
            pool.wait_ge(s_const, FILLS)
            nc.gpsimd.memset(go_on[:, :, 0:1], 0.0).then_inc(s_const, 1)
            for n, row in enumerate((0, E)):
                pool.wait_ge(s_const, FILLS + 1 + n)
                nc.gpsimd.memset(pick_c[row:row + 1, :].bitcast(F32), 1.0).then_inc(s_const, 1)
            pool.wait_ge(s_const, FILLS + 3)
            nc.gpsimd.affine_select(out=ident[:], in_=ident[:], compare_op=ALU.not_equal, fill=1.0,
                                    base=0, pattern=[[-1, P]], channel_multiplier=1).then_inc(s_const, 1)
            pool.wait_ge(s_wload, 16 * WLOADS)
            pool.wait_ge(s_const, CONSTS)

            def mean(t0, par, s_rows, total, s_mean, minus_mean, shift_sq, s_shift):
                if not isinstance(t0, int) or t0 >= 3:
                    pool.wait_ge(s_shift, t0 - 2)
                pool.wait_ge(s_rows, t0)
                nc.gpsimd.tensor_tensor(shift_sq[:, par:par + 1], total[:, par:par + 1], per_row_sq[:],
                                        ALU.mult).then_inc(s_mean, 1)
                nc.gpsimd.tensor_tensor(minus_mean[:, par:par + 1], total[:, par:par + 1], per_row[:],
                                        ALU.mult).then_inc(s_mean, 1)

            def norm(t0, par, s_var, var, s_ve, ve, s_mean, minus_mean, s_rstd, rstd, s_shift, shift, s_used):
                if not isinstance(t0, int) or t0 >= 2:
                    pool.wait_ge(s_rstd, t0 - 1)
                pool.wait_ge(s_var, t0)
                nc.gpsimd.tensor_tensor(ve[:], var[:, par:par + 1], eps[:], ALU.add).then_inc(s_ve, 1)
                if not isinstance(t0, int) or t0 >= 3:
                    pool.wait_ge(s_used, t0 - 2)
                    pool.wait_ge(s_shift, t0 - 2)
                pool.wait_ge(s_ve, t0)
                nc.gpsimd.tensor_tensor(rstd[:, par:par + 1], ve[:], minus_half[:], ALU.pow).then_inc(s_rstd, 1)
                pool.wait_ge(s_mean, 2 * t0)
                pool.wait_ge(s_rstd, t0)
                nc.gpsimd.tensor_tensor(shift[:, par:par + 1], minus_mean[:, par:par + 1], rstd[:, par:par + 1],
                                        ALU.mult).then_inc(s_shift, 1)

            def fold(s_in, t1, row, s_out):
                halves = by_head(row[:]).rearrange("p h (a s) -> p h a s", a=2)
                pool.wait_ge(s_in, t1)
                nc.gpsimd.tensor_tensor(halves[:, :, 0, :], halves[:, :, 0, :], halves[:, :, 1, :],
                                        ALU.add).then_inc(s_out, 1)

            def slot(turn, j):
                base = turn * UNROLL
                if in_range(turn, j, LAG_Y):
                    i = j - LAG_Y
                    norm(base + i + 1, i % 2, s_var1, var1, s_ve1, ve1, s_mean1, minus_mean1, s_rstd1, rstd1,
                         s_shift1, shift1, s_y)
                if in_range(turn, j, LAG_FINAL):
                    i = j - LAG_FINAL
                    norm(base + i + 1, i % 2, s_var2, var2, s_ve2, ve2, s_mean2, minus_mean2, s_rstd2, rstd2,
                         s_shift2, shift2, s_final)
                if in_range(turn, j, LAG_SPLIT) and (j - LAG_SPLIT) % GROUP == 0:
                    i = j - LAG_SPLIT
                    pool.wait_ge(s_acchi, group_of(turn, i) + 1)
                    nc.gpsimd.tensor_tensor(acc_lo[:], acc[:], acc_hi[:].bitcast(F32),
                                            ALU.subtract).then_inc(s_acclo, 1)
                if in_range(turn, j, LAG_NORM1):
                    i = j - LAG_NORM1
                    mean(base + i + 1, i % 2, s_r1, sum1, s_mean1, minus_mean1, shift_sq1, s_shift1)
                if in_range(turn, j, LAG_NORM2):
                    i = j - LAG_NORM2
                    mean(base + i + 1, i % 2, s_r2, sum2, s_mean2, minus_mean2, shift_sq2, s_shift2)
                if in_range(turn, j, LAG_XB):
                    i = j - LAG_XB
                    pool.wait_ge(s_xr[i % YR], 32 * (turns_of(turn, j, LAG_XB, YR) + 1))
                    nc.gpsimd.tensor_tensor(y_sb[:, i % YR, :], y_sb[:, i % YR, :], bo_bc[:],
                                            ALU.add).then_inc(s_xb, 1)
                if in_range(turn, j, LAG_YT):
                    i = j - LAG_YT
                    pool.wait_ge(s_yT, base + i + 1)
                    nc.gpsimd.tensor_tensor(y_sb[:, i % YR, :], y_sb[:, i % YR, :], bout_bc[:],
                                            ALU.add).then_inc(s_yb, 1)
                if in_range(turn, j, LAG_STEP) and pool_steps(turn, j):
                    i = j - LAG_STEP
                    pool.wait_ge(s_step2, base + i + 1)
                    if not isinstance(base, int) or base + i >= UR:
                        pool.wait_ge(s_uT, base + (i - i % GROUP) - UR + GROUP)
                    nc.gpsimd.tensor_tensor(u_of(i), by_head(u_raw[:, i % 2, :]), spread(step[:]),
                                            ALU.add).then_inc(s_u, 1)
                if in_range(turn, j, LAG_SIDE):
                    i = j - LAG_SIDE
                    fold(s_side, base + i + 1, side, s_foldc)
                    fold(s_above, base + i + 1, above, s_folds)

            slots(pool, slot)

        STEPS = ([("kpT", c) for c in range(C)] + [("keysT", c) for c in range(C)]
                 + [("WqT", c) for c in range(C)] + [("A", c) for c in range(C)] + [("c", 0), ("V", 0)])

        def done(name):
            return max(i for i, (n, _) in enumerate(STEPS) if n == name) + 1

        @block.tensor
        def _(pe):
            pe.wait_ge(s_wkeys, 16 * KEY_LOADS)
            pe.wait_ge(s_const, CONSTS)
            for n, (name, c) in enumerate(STEPS):
                ps = banks[n % 8]
                if n >= 8:
                    pe.wait_ge(s_sev, n - 7)
                here = slice(c * P, (c + 1) * P)
                if name == "kpT":
                    mm = nc.tensor.transpose(ps[:, 0:S], kp_sb[:, here], ident[0:S, 0:S])
                elif name == "keysT":
                    if c == 0:
                        pe.wait_ge(s_sev, done("kpT"))
                    for d in range(C):
                        mm = nc.tensor.matmul(ps[:, 0:P], Wk_sb[:, d, here], kpT4[:, d, :],
                                              start=(d == 0), stop=(d == C - 1))
                elif name == "V":
                    pe.wait_ge(s_sev, done("keysT"))
                    pe.wait_ge(s_wload, 16 * WLOADS)
                    for d in range(C):
                        nc.tensor.matmul(ps[:], keysT4[:, d, :], Wv_sb[:, d, :], start=(d == 0), stop=False)
                    mm = nc.tensor.matmul(ps[:], ones_row, bv_row, start=False, stop=True)
                elif name == "WqT":
                    if c == 0:
                        pe.wait_ge(s_wq, 16 * Q_LOADS)
                    for d in range(C):
                        mm = nc.tensor.transpose(ps[:, d * P:(d + 1) * P], Wq_sb[:, d, here], ident[:])
                elif name == "c":
                    for k in range(C):
                        mm = nc.tensor.matmul(ps[0:1, k * P:(k + 1) * P], bq_c[:, k:k + 1], K_blk[:, k, :],
                                              start=True, stop=True)
                else:
                    if c == 0:
                        pe.wait_ge(s_blk, C)
                        pe.wait_ge(s_sev, done("WqT"))
                    for k in range(C):
                        mm = nc.tensor.matmul(ps[:, k * P:(k + 1) * P], WqT[:, k, here], K_blk[:, k, :],
                                              start=True, stop=True)
                mm.then_inc(s_smm, 1)
            pe.wait_ge(s_ready, 2 * C)
            pe.wait_ge(s_c, 2)
            pe.wait_ge(s_sev, len(STEPS))

            def three_pass(ps, hi, lo, w_hi, w_lo, start):
                for c in range(C):
                    nc.tensor.matmul(ps[:], hi[:, c, :], w_hi[:, c, :], start=start and c == 0, stop=False)
                    nc.tensor.matmul(ps[:], hi[:, c, :], w_lo[:, c, :], start=False, stop=False)
                    mm = nc.tensor.matmul(ps[:], lo[:, c, :], w_hi[:, c, :], start=False, stop=(c == C - 1))
                return mm

            def probabilities(turn, j, half):
                for lead, b in batches(turn, j, half):
                    base = turn * UNROLL
                    if b == 0:
                        pe.wait_ge(s_checked, group_of(turn, lead) + 1)
                    if not isinstance(turn, int) or base + lead + b >= 1:
                        pe.wait_ge(s_p, base + lead + b)
                    for a in range(HPC):
                        mm = nc.tensor.transpose(
                            uT_ps[:, a * P:(a + 1) * P],
                            u_sb[:, lead // GROUP % 2, HPC * b + a].rearrange("p g s -> p (g s)"), ident[:])
                    mm.then_inc(s_uT, 1)

            def slot(turn, j):
                base = turn * UNROLL
                if in_range(turn, j, LAG_SCORE):
                    i = j - LAG_SCORE
                    pe.wait_ge(s_xhi, base + i + 1)
                    pe.wait_ge(s_xlo, base + i + 1)
                    if not isinstance(turn, int) or base + i >= 2:
                        pe.wait_ge(s_u1, base + i - 1)
                    z = z_ps[i % 2]
                    nc.tensor.matmul(z[:], pick_c[:], bias_rows[:], start=True, stop=False)
                    three_pass(z, xT_hi, xT_lo, A_hi, A_lo, start=False).then_inc(s_score, 1)
                lead = j - LAG_CHECK
                if lead % GROUP == 0 and in_range(turn, j, LAG_CHECK):
                    pe.wait_ge(s_differs, group_of(turn, lead) + 1)
                    if not isinstance(turn, int) or base + lead > 0:
                        pe.wait_ge(s_p, base + lead)
                    nc.tensor.matmul(uT_ps[0:1, 0:GROUP], ones_col[:], differs[:], start=True,
                                     stop=True).then_inc(s_opens, 1)
                if in_range(turn, j, LAG_X):
                    i = j - LAG_X
                    pe.wait_ge(s_x[i % XR], 16 * (turns_of(turn, j, LAG_X, XR) + 1))
                    if not isinstance(turn, int) or base + i >= 1:
                        pe.wait_ge(s_xhi, base + i)
                        pe.wait_ge(s_xlo, base + i)
                    for c in range(C):
                        mm = nc.tensor.transpose(xT_ps[:, c * P:(c + 1) * P], x_sb[:, i % XR, c * P:(c + 1) * P],
                                                 ident[:])
                    mm.then_inc(s_xT, 1)
                if in_range(turn, j, LAG_YT):
                    i = j - LAG_YT
                    pe.wait_ge(s_y, base + i + 1)
                    if not isinstance(turn, int) or base + i >= 1:
                        pe.wait_ge(s_sc, 2 * (base + i))
                    for c in range(C):
                        mm = nc.tensor.transpose(ys_ps[:, c * P:(c + 1) * P], y_sb[:, i % YR, c * P:(c + 1) * P],
                                                 ident[:])
                    mm.then_inc(s_yT, 1)
                probabilities(turn, j, 0)
                if in_range(turn, j, LAG_WO):
                    i = j - LAG_WO
                    if isinstance(turn, int) and base + i == 0:
                        pe.wait_ge(s_ready, 2 * C + 2)
                    pe.wait_ge(s_ohi, base + i + 1)
                    pe.wait_ge(s_olo, base + i + 1)
                    if not isinstance(turn, int) or base + i >= 1:
                        pe.wait_ge(s_r1, base + i)
                    three_pass(o_ps, oT_hi, oT_lo, Wo_hi, Wo_lo, start=True).then_inc(s_o, 1)
                if in_range(turn, j, LAG_VALUE):
                    i = j - LAG_VALUE
                    if i % UNROLL == 0:
                        pe.wait_ge(s_p, base + i + UNROLL)
                    if not isinstance(turn, int) or base + i >= 1:
                        pe.wait_ge(s_olo, base + i)
                    nc.tensor.matmul(v_ps[:], V_blk[:, i % H, :],
                                     pT[:, bass.ds(pair_place(turn, i) + i % H * C * P, C * P)],
                                     start=True, stop=True).then_inc(s_v, 1)
                if in_range(turn, j, LAG_YT):
                    i = j - LAG_YT
                    pe.wait_ge(s_yTc, base + i + 1)
                    for c in range(C):
                        mm = nc.tensor.matmul(ys_ps[0:M, 0:P], Win_sb[:, c, :], yT[:, c, :], start=(c == 0),
                                              stop=(c == C - 1))
                    mm.then_inc(s_s, 1)
                probabilities(turn, j, 1)
                if in_range(turn, j, LAG_OUT):
                    i = j - LAG_OUT
                    if i % GROUP == 0:
                        pe.wait_ge(s_acclo, group_of(turn, i) + 1)
                        if isinstance(turn, int) and base + i == 0:
                            pe.wait_ge(s_ready, 2 * C + 4)
                    if not isinstance(turn, int) or base + i >= 1:
                        pe.wait_ge(s_r2, base + i)
                    here = slice(i % GROUP * P, (i % GROUP + 1) * P)
                    nc.tensor.matmul(f_ps[:], acc_hi[:, here], Wout_hi[:], start=True, stop=False)
                    nc.tensor.matmul(f_ps[:], acc_hi[:, here], Wout_lo[:], start=False, stop=False)
                    nc.tensor.matmul(f_ps[:], acc_lo[:, here], Wout_hi[:], start=False, stop=True).then_inc(s_f, 1)

            slots(pe, slot)

        @block.scalar
        def _(act):
            for n, (name, c) in enumerate(STEPS):
                ps = banks[n % 8]
                act.wait_ge(s_smm, n + 1)
                if name == "kpT":
                    for a in range(HPC):
                        cp = nc.scalar.copy(kpT4[:, c, a * S:(a + 1) * S], ps[:, 0:S])
                    cp.then_inc(s_sev, 1)
                elif name == "keysT":
                    nc.scalar.activation(keysT4[:, c, :], ps[:, 0:P], ACT.Identity,
                                         bias=bk_c[:, c:c + 1]).then_inc(s_sev, 1)
                elif name == "V":
                    act.wait_ge(s_const, CONSTS)
                    for a in range(HPC):
                        rows = slice(a * S, (a + 1) * S)
                        cp = nc.scalar.copy(V_blk[rows, :, rows], ps[rows, :].rearrange("p (h d) -> p h d", h=H))
                    cp.then_inc(s_sev, 1)
                elif name == "WqT":
                    nc.scalar.copy(WqT[:, c, :], ps[:]).then_inc(s_sev, 1)
                elif name == "c":
                    nc.scalar.mul(c_full, ps[0:1, :], SCALE).then_inc(s_sev, 1)
                else:
                    nc.scalar.mul(A_f[:, c, :], ps[:], SCALE).then_inc(s_sev, 1)

            def probabilities(turn, j, half):
                for lead, b in batches(turn, j, half):
                    base = turn * UNROLL
                    jc, h0 = (lead // GROUP) % C, HPC * b
                    act.wait_ge(s_uT, base + lead + b + 1)
                    if not isinstance(turn, int) or base + lead >= 2 * UNROLL:
                        act.wait_ge(s_v, base + (lead - lead % UNROLL) - 2 * UNROLL + h0 + HPC)
                    place = pT[:, bass.ds(pair_place(turn, lead) + h0 * C * P, HPC * C * P)]
                    nc.scalar.activation(place.rearrange("p (a c n) -> p a c n", a=HPC, c=C)[:, :, jc, :],
                                         uT_ps[:].rearrange("p (a n) -> p a n", a=HPC),
                                         ACT.Relu).then_inc(s_p, 1)

            def square(turn, j, lag, s_mean, s_before, n_before, shift_sq, s_ve, var, s_var):
                i = j - lag
                t0 = turn * UNROLL + i + 1
                act.wait_ge(s_mean, 2 * t0)
                if not isinstance(t0, int) or t0 >= 3:
                    act.wait_ge(s_ve, t0 - 2)
                if not isinstance(n_before, int) or n_before > 0:
                    act.wait_ge(s_before, n_before)
                nc.scalar.activation(unread[:], y_sb[:, i % YR, :], ACT.Square,
                                     bias=shift_sq[:, i % 2:i % 2 + 1], scale=1.0 / D ** 0.5,
                                     accum_out=var[:, i % 2:i % 2 + 1]).then_inc(s_var, 1)

            def make_hinge(turn, j, half):
                i = j - LAG_HINGE
                lead = i - i % GROUP
                if not in_range(turn, 0, -lead):
                    return
                base, g, k = turn * UNROLL, group_of(turn, lead), 2 * (i % GROUP) + half
                if k == 0:
                    act.wait_ge(s_sc, 2 * (base + lead + GROUP))
                if not isinstance(turn, int) or base + lead > 0 or k >= HR:
                    act.wait_ge(s_acc, g * KH + k - HR + 1)
                nc.scalar.activation(hinge[:, k % HR, :], s_sb[:, (lead // GROUP) % 2, :], ACT.Relu,
                                     bias=b1c[:, k:k + 1], scale=w1c[:, k:k + 1]).then_inc(s_hinge, 1)

            def slot(turn, j):
                base = turn * UNROLL
                if in_range(turn, j, LAG_WO):
                    i = j - LAG_WO
                    act.wait_ge(s_v, base + i + 1)
                    if not isinstance(turn, int) or base + i >= 1:
                        act.wait_ge(s_o, base + i)
                    nc.scalar.copy(oT_hi[:].rearrange("p c n -> p (c n)"), v_ps[:]).then_inc(s_ohi, 1)
                if in_range(turn, j, LAG_S):
                    i = j - LAG_S
                    par, q = (i // GROUP) % 2, i % GROUP
                    act.wait_ge(s_s, base + i + 1)
                    if not isinstance(turn, int) or base + i >= 2 * GROUP:
                        act.wait_ge(s_hinge, (group_of(turn, i) - 1) * KH)
                    for half in (slice(0, M), slice(M, P)):
                        nc.scalar.activation(s_sb[half, par, q * P:(q + 1) * P], ys_ps[0:M, 0:P], ACT.Identity,
                                             bias=bin_sb[:]).then_inc(s_sc, 1)
                if in_range(turn, j, LAG_SPLIT) and (j - LAG_SPLIT) % GROUP == 0:
                    i = j - LAG_SPLIT
                    act.wait_ge(s_acc, (group_of(turn, i) + 1) * KH)
                    if not isinstance(turn, int) or base + i > 0:
                        act.wait_ge(s_f, base + i)
                    nc.scalar.copy(acc_hi[:], acc[:]).then_inc(s_acchi, 1)
                if in_range(turn, j, LAG_COUNT):
                    i = j - LAG_COUNT
                    act.wait_ge(s_u, base + i + 1)
                    if (not isinstance(turn, int) or base + i >= UR) and i % GROUP == 0:
                        act.wait_ge(s_differs, group_of(turn, i) - 1)
                    if not isinstance(turn, int) or base + i >= 1:
                        act.wait_ge(s_count2, base + i)
                    for s_var, lag in ((s_var1, LAG_NORM1), (s_var2, LAG_NORM2)):
                        squares = so_far(turn, j - 1, lag)
                        if not isinstance(turn, int) or squares > 0:
                            act.wait_ge(s_var, squares)
                    nc.scalar.activation(by_head(unread[:]), u_of(i), ACT.Sign,
                                         accum_out=count2[:, i % UR:i % UR + 1]).then_inc(s_count2, 1)
                if in_range(turn, j, LAG_FINAL) and not vector_finishes(turn):
                    i = j - LAG_FINAL
                    act.wait_ge(s_shift2, base + i + 1)
                    if not isinstance(turn, int) or base + i >= OR:
                        act.wait_ge(s_store[i % OR], 32 * turns_of(turn, j, LAG_FINAL, OR))
                    nc.scalar.activation(o_sb[:, i % OR, :], y_sb[:, i % YR, :], ACT.Identity,
                                         bias=shift2[:, i % 2:i % 2 + 1], scale=rstd2[:, i % 2:i % 2 + 1]
                                         ).then_inc(s_final, 1)
                if in_range(turn, j, LAG_Y):
                    i = j - LAG_Y
                    act.wait_ge(s_shift1, base + i + 1)
                    nc.scalar.activation(y_sb[:, i % YR, :], y_sb[:, i % YR, :], ACT.Identity,
                                         bias=shift1[:, i % 2:i % 2 + 1], scale=rstd1[:, i % 2:i % 2 + 1]
                                         ).then_inc(s_y, 1)
                if in_range(turn, j, LAG_X):
                    i = j - LAG_X
                    act.wait_ge(s_xT, base + i + 1)
                    if not isinstance(turn, int) or base + i >= 1:
                        act.wait_ge(s_score, base + i)
                    nc.scalar.copy(xT_hi[:].rearrange("p c n -> p (c n)"), xT_ps[:]).then_inc(s_xhi, 1)
                if in_range(turn, j, LAG_YT):
                    i = j - LAG_YT
                    act.wait_ge(s_yT, base + i + 1)
                    if not isinstance(turn, int) or base + i >= 1:
                        act.wait_ge(s_s, base + i)
                    nc.scalar.copy(yT[:].rearrange("p c n -> p (c n)"), ys_ps[:]).then_inc(s_yTc, 1)
                probabilities(turn, j, 0)
                if in_range(turn, j, LAG_SIDE):
                    i = j - LAG_SIDE
                    act.wait_ge(s_u1, base + i + 1)
                    if not isinstance(turn, int) or base + i >= 1:
                        act.wait_ge(s_sums, base + i)
                        act.wait_ge(s_sumc, base + i)
                    if (not isinstance(turn, int) or base + i >= UR) and i % GROUP == 0:
                        act.wait_ge(s_differs, group_of(turn, i) - 1)
                    nc.scalar.activation(side[:], u_raw[:, i % 2, :], ACT.Sign,
                                         accum_out=count1[:, i % UR:i % UR + 1]).then_inc(s_side, 1)
                    nc.scalar.activation(above[:], u_raw[:, i % 2, :], ACT.Relu).then_inc(s_above, 1)
                if in_range(turn, j, LAG_NORM1):
                    square(turn, j, LAG_NORM1, s_mean1, s_count2, so_far(turn, j, LAG_COUNT), shift_sq1, s_ve1,
                           var1, s_var1)
                make_hinge(turn, j, 0)
                if in_range(turn, j, LAG_NORM2):
                    square(turn, j, LAG_NORM2, s_mean2, s_var1, so_far(turn, j, LAG_NORM1), shift_sq2, s_ve2,
                           var2, s_var2)
                make_hinge(turn, j, 1)
                probabilities(turn, j, 1)

            slots(act, slot)

        @block.vector
        def _(dve):
            dve.wait_ge(s_const, CONSTS)
            dve.wait_ge(s_sev, done("keysT"))
            for c in range(C):
                for a in range(HPC):
                    rows = slice(a * S, (a + 1) * S)
                    cp = nc.vector.tensor_copy(K_blk[rows, c, rows], keysT4[rows, c, 0:S])
                cp.then_inc(s_blk, 1)
            for c in range(C):
                dve.wait_ge(s_sev, done("WqT") + c + 1)
                nc.vector.tensor_copy(A_hi[:, c, :], A_f[:, c, :]).then_inc(s_ready, 1)
                dve.wait_ge(s_ready, 2 * c + 1)
                nc.vector.tensor_tensor(A_lo[:, c, :], A_f[:, c, :], A_hi[:, c, :].bitcast(F32),
                                        ALU.subtract).then_inc(s_ready, 1)
            dve.wait_ge(s_sev, done("c"))
            nc.vector.tensor_copy(bias_rows[0:1, :], c_full).then_inc(s_c, 1)
            dve.wait_ge(s_c, 1)
            nc.vector.tensor_tensor(bias_rows[E:E + 1, :], c_full, bias_rows[0:1, :].bitcast(F32),
                                    ALU.subtract).then_inc(s_c, 1)
            dve.wait_ge(s_wload, 16 * WLOADS)
            nc.vector.tensor_copy(Wo_hi[:], Wo_sb).then_inc(s_ready, 1)
            dve.wait_ge(s_ready, 2 * C + 1)
            nc.vector.tensor_tensor(Wo_lo[:], Wo_sb, Wo_hi[:].bitcast(F32), ALU.subtract).then_inc(s_ready, 1)
            nc.vector.tensor_copy(Wout_hi[:], Wout_sb).then_inc(s_ready, 1)
            dve.wait_ge(s_ready, 2 * C + 3)
            nc.vector.tensor_tensor(Wout_lo[:], Wout_sb, Wout_hi[:].bitcast(F32), ALU.subtract).then_inc(s_ready, 1)

            def sort_tile(par, q):
                with dve.Fori(0, H // HPC) as quarter:
                    block = u_flat[:, bass.ds(quarter * (HPC * GROUP * S) + par * (H * GROUP * S), HPC * GROUP * S)]
                    scores = block.rearrange("p (h g s) -> p h g s", h=HPC, g=GROUP)[:, :, q, :]
                    nc.vector.tensor_copy(rest, scores)
                    dve.drain()
                    for r in range(0, S, TOP):
                        for a in range(HPC):
                            nc.vector.max(ranked[:, a, r:r + TOP], rest[:, a, :])
                        dve.drain()
                        for a in range(HPC if r + TOP < S else 0):
                            nc.vector.match_replace(rest[:, a, :], ranked[:, a, r:r + TOP], rest[:, a, :], LOWEST)
                        dve.drain()
                    for a in range(HPC):
                        nc.vector.tensor_tensor_scan(rest[:, a, :], ones_s[:], ranked[:, a, :], 0.0, ALU.mult,
                                                     ALU.add)
                    dve.drain()
                    nc.vector.scalar_tensor_tensor(rest, rest, -1.0, rank_inv[:].unsqueeze(1).broadcast_to(
                        [P, HPC, S]), ALU.add, ALU.mult)
                    dve.drain()
                    nc.vector.tensor_reduce(tau_some[:], rest, AX.X, ALU.max)
                    dve.drain()
                    nc.vector.scalar_tensor_tensor(scores, tau_some[:].unsqueeze(2).broadcast_to([P, HPC, S]), -1.0,
                                                   scores, ALU.mult, ALU.add)
                    dve.drain()

            def residual(t1, ps, s_prod, other, s_other, n_other, rows, total, s_mean, s_rows):
                dve.wait_ge(s_prod, t1)
                dve.wait_ge(s_other, n_other)
                if not isinstance(t1, int) or t1 >= 3:
                    dve.wait_ge(s_mean, 2 * t1 - 4)
                nc.vector.scalar_tensor_tensor(rows, ps[:], 0.0, other, ALU.add, ALU.add,
                                               accum_out=total).then_inc(s_rows, 1)

            def lower_half(row):
                return by_head(row[:])[:, :, 0:S // 2]

            def slot(turn, j):
                base = turn * UNROLL
                lead = j - LAG_CHECK
                checks = lead % GROUP == 0 and in_range(turn, j, LAG_CHECK)
                if in_range(turn, j, LAG_WO):
                    i = j - LAG_WO
                    dve.wait_ge(s_ohi, base + i + 1)
                    nc.vector.tensor_tensor(
                        oT_lo[:].rearrange("p c n -> p (c n)"), v_ps[:],
                        oT_hi[:].bitcast(F32).rearrange("p c n -> p (c n)"), ALU.subtract
                    ).then_inc(s_olo, 1)
                if checks:
                    g = group_of(turn, lead)
                    dve.wait_ge(s_count2, base + lead + GROUP)
                    if not isinstance(turn, int) or base + lead > 0:
                        dve.wait_ge(s_opens, g)
                    places = slice(lead % UR, lead % UR + GROUP)
                    nc.vector.tensor_tensor(differs[:], count1[:, places], count2[:, places],
                                            ALU.not_equal).then_inc(s_differs, 1)
                if in_range(turn, j, LAG_STEP):
                    t1 = base + (j - LAG_STEP) + 1
                    dve.wait_ge(s_foldc, t1)
                    nc.vector.tensor_reduce(sum_side[:], lower_half(side), AX.X, ALU.add).then_inc(s_sumc, 1)
                    dve.wait_ge(s_folds, t1)
                    nc.vector.tensor_reduce(sum_above[:], lower_half(above), AX.X, ALU.add).then_inc(s_sums, 1)
                    dve.wait_ge(s_sumc, t1)
                    nc.vector.tensor_scalar(twice[:], sum_side[:], float(S), 2.0, ALU.add, ALU.max).then_inc(s_twice, 1)
                if in_range(turn, j, LAG_NORM1):
                    i = j - LAG_NORM1
                    residual(base + i + 1, o_ps, s_o, y_sb[:, i % YR, :], s_xb, base + i + 1, y_sb[:, i % YR, :],
                             sum1[:, i % 2:i % 2 + 1], s_mean1, s_r1)
                if in_range(turn, j, LAG_STEP):
                    t1 = base + (j - LAG_STEP) + 1
                    dve.wait_ge(s_twice, t1)
                    nc.vector.reciprocal(twice_inv[:], twice[:]).then_inc(s_inv, 1)
                if in_range(turn, j, LAG_NORM2):
                    i = j - LAG_NORM2
                    residual(base + i + 1, f_ps, s_f, y_sb[:, i % YR, :], s_yb, base + i + 1,
                             y_sb[:, i % YR, :], sum2[:, i % 2:i % 2 + 1], s_mean2, s_r2)
                if in_range(turn, j, LAG_FINAL) and vector_finishes(turn):
                    i = j - LAG_FINAL
                    dve.wait_ge(s_final, base + i)
                    dve.wait_ge(s_shift2, base + i + 1)
                    dve.wait_ge(s_store[i % OR], 32 * turns_of(turn, j, LAG_FINAL, OR))
                    nc.vector.tensor_scalar(o_sb[:, i % OR, :], y_sb[:, i % YR, :], rstd2[:, i % 2:i % 2 + 1],
                                            shift2[:, i % 2:i % 2 + 1], ALU.mult, ALU.add).then_inc(s_final, 1)
                if in_range(turn, j, LAG_STEP):
                    t1 = base + (j - LAG_STEP) + 1
                    dve.wait_ge(s_sums, t1)
                    dve.wait_ge(s_inv, t1)
                    if not isinstance(t1, int) or t1 > 1:
                        dve.wait_ge(s_u, t1 - 1)
                    nc.vector.scalar_tensor_tensor(step[:], sum_above[:], -1.0, twice_inv[:], ALU.add,
                                                   ALU.mult).then_inc(s_step, 1)
                if in_range(turn, j, LAG_STEP):
                    i = j - LAG_STEP
                    dve.wait_ge(s_step, base + i + 1)
                    if pool_steps(turn, j):
                        nc.vector.tensor_scalar(step[:], step[:], -2.0, None, ALU.mult).then_inc(s_step2, 1)
                    else:
                        if not isinstance(base, int) or base + i >= UR:
                            dve.wait_ge(s_uT, base + (i - i % GROUP) - UR + GROUP)
                        nc.vector.scalar_tensor_tensor(u_of(i), spread(step[:]), -2.0, by_head(u_raw[:, i % 2, :]),
                                                       ALU.mult, ALU.add).then_inc(s_u, 1)
                if in_range(turn, j, LAG_SCORE) and not isinstance(turn, int):
                    dve.wait_ge(s_score, base + (j - LAG_SCORE) + 1)
                if in_range(turn, j, LAG_X):
                    i = j - LAG_X
                    dve.wait_ge(s_xhi, base + i + 1)
                    nc.vector.tensor_tensor(
                        xT_lo[:].rearrange("p c n -> p (c n)"), xT_ps[:],
                        xT_hi[:].bitcast(F32).rearrange("p c n -> p (c n)"), ALU.subtract
                    ).then_inc(s_xlo, 1)
                if checks:
                    g = group_of(turn, lead)
                    dve.wait_ge(s_opens, g + 1)
                    nc.vector.tensor_reduce(open_any[:], uT_ps[0:1, 0:GROUP], AX.X, ALU.max)
                    dve.drain()
                    with dve.If(dve.value_load(open_any[:], min_val=0, max_val=P) > 0):
                        nc.vector.tensor_copy(open_tiles[:], uT_ps[0:1, 0:GROUP])
                        dve.drain()
                        for q in range(GROUP):
                            with dve.If(dve.value_load(open_tiles[:, q:q + 1], min_val=0, max_val=P) > 0):
                                sort_tile(lead // GROUP % 2, q)
                    dve.nop().then_inc(s_checked, 1)
                if in_range(turn, j, LAG_SCORE):
                    i = j - LAG_SCORE
                    if isinstance(turn, int):
                        dve.wait_ge(s_score, base + i + 1)
                    for h in range(H):
                        mx = nc.vector.max(top8[:, h, :], z_ps[i % 2][:, h * S:(h + 1) * S])
                    mx.then_inc(s_top, 1)
                if in_range(turn, j, LAG_SCORE):
                    i = j - LAG_SCORE
                    dve.wait_ge(s_top, base + i + 1)
                    nc.vector.tensor_tensor_scan(cum[:].rearrange("p h k -> p (h k)"),
                                                 go_on[:].rearrange("p h k -> p (h k)"),
                                                 top8[:].rearrange("p h k -> p (h k)"), 0.0,
                                                 ALU.mult, ALU.add).then_inc(s_cum, 1)
                hinge_step(turn, j, 0)
                if in_range(turn, j, LAG_SCORE):
                    i = j - LAG_SCORE
                    dve.wait_ge(s_cum, base + i + 1)
                    nc.vector.scalar_tensor_tensor(cum[:], cum[:], -1.0, rank_inv[:, 0:TOP].unsqueeze(1).broadcast_to([P, H, TOP]), ALU.add,
                                                   ALU.mult).then_inc(s_cand, 1)
                hinge_step(turn, j, 1)
                if in_range(turn, j, LAG_SCORE):
                    i = j - LAG_SCORE
                    dve.wait_ge(s_cand, base + i + 1)
                    nc.vector.tensor_reduce(tau[:], cum[:], AX.X, ALU.max).then_inc(s_tau, 1)
                    dve.wait_ge(s_tau, base + i + 1)
                    if not isinstance(base, int) or base + i >= 2:
                        dve.wait_ge(s_u, base + i - 1)
                    nc.vector.tensor_tensor(by_head(u_raw[:, i % 2, :]), by_head(z_ps[i % 2][:]),
                                            spread(tau[:]), ALU.subtract).then_inc(s_u1, 1)

            def hinge_step(turn, j, half):
                base = turn * UNROLL
                i = j - LAG_HINGE
                first = i - i % GROUP
                if not in_range(turn, 0, -first):
                    return
                g, k = group_of(turn, first), 2 * (i % GROUP) + half
                dve.wait_ge(s_hinge, g * KH + k + 1)
                if k == 0:
                    if not isinstance(base, int) or base + first > 0:
                        dve.wait_ge(s_acclo, g)
                    nc.vector.tensor_scalar(acc[:], hinge[:, k % HR, :], w2c[:, k:k + 1], b2c[:],
                                            ALU.mult, ALU.add).then_inc(s_acc, 1)
                else:
                    dve.wait_ge(s_acc, g * KH + k)
                    nc.vector.scalar_tensor_tensor(acc[:], hinge[:, k % HR, :], w2c[:, k:k + 1],
                                                   acc[:], ALU.mult, ALU.add).then_inc(s_acc, 1)

            slots(dve, slot)


_INS = ['query', 'key_param', 'Wq', 'bq', 'Wk', 'bk', 'Wv', 'bv', 'Wo', 'bo']
_FFN = ['Win', 'bin_', 'W1', 'b1', 'W2', 'b2', 'Wout', 'bout']
_NAMES = ['L0_attn_' + n for n in _INS] + ['L0_ffn_' + n for n in _FFN]
_OUTS = [((16, 1024, 512), 'float32')]


def kernel(**inputs):
    import numpy as _np
    import concourse.bacc as _bacc
    from concourse import mybir as _mybir
    from concourse.bass_utils import run_bass_kernel_spmd as _run

    nc = _bacc.Bacc("TRN2", target_bir_lowering=False, num_devices=1)
    arrays, args = {}, []
    for name in _NAMES:
        a = _np.ascontiguousarray(inputs[name])
        arrays[f"in_{name}_dram"] = a
        args.append(nc.dram_tensor(f"in_{name}_dram", a.shape, _mybir.dt.from_np(a.dtype), kind="ExternalInput").ap())
    for i, (shape, dtype) in enumerate(_OUTS):
        dt = _mybir.dt.from_np(_np.dtype(dtype))
        args.append(nc.dram_tensor(f"out_{i}_dram", shape, dt, kind="ExternalOutput").ap())
    build_kernel(nc, *args)
    r = _run(nc, [arrays], core_ids=[0])
    got = tuple(r.results[0][f"out_{i}_dram"] for i in range(len(_OUTS)))
    return got[0]
```
